# Optimizing a Trainium2 kernel written in Bass

```python
import numpy as np
import jax
import jax.numpy as jnp

def _softmax(x, axis=-1):
    return jax.nn.softmax(x, axis=axis)

def _gelu(x):
    return jax.nn.gelu(x, approximate=True)

def _silu(x):
    return jax.nn.silu(x)

def _sigmoid(x):
    return jax.nn.sigmoid(x)

def _layernorm(x, axis=-1, eps=1e-05):
    m = jnp.mean(x, axis=axis, keepdims=True)
    v = jnp.var(x, axis=axis, keepdims=True)
    return (x - m) / jnp.sqrt(v + eps)

def _scatter_add(tgt, idx, src, axis=0):
    return tgt.at[idx].add(src)

def _segment_sum(src, seg, n):
    return jax.ops.segment_sum(src, seg, n)
kernel_name = 'mk_vit_tower_d1_tok_img4096_r4_0917ee'

def setup_inputs(seed: int=0):
    np.random.seed(seed)
    _w = jnp.asarray

    def _rec_inputs():
        import jax
        import jax.numpy as jnp
        _rk = jax.random.key(seed)
        x = -0.0064186 + 0.999588 * jax.random.normal(jax.random.fold_in(_rk, 1), (64, 128, 64, 2), jnp.float32)
        return x
    x = _rec_inputs()

    def _L0_tok_setup():
        import jax, jax.numpy as jnp
        import numpy as np
        import math
        H, N, C, L_VAL = (128, 64, 1, 1024)
        EPS = 1e-07

        def _reciprocal(x, epsilon):
            xc = jnp.conj(x)
            return xc / (x * xc + epsilon)
        key = jax.random.key(seed)
        k1, k2, k3 = jax.random.split(key, 3)
        log_dt = math.log(0.001) + jax.random.uniform(k1, (H,), dtype=jnp.float32) * (math.log(0.1) - math.log(0.001))
        log_dt = jnp.tile(log_dt[:, None], (1, 2))
        lam_im = jax.random.normal(k2, (N,), dtype=jnp.float32)
        Lambda = jnp.stack([-0.5 * jnp.ones((N,), jnp.float32), lam_im], axis=-1)
        W = jax.random.normal(k3, (C, H, N, 2), dtype=jnp.float32)
        return {'log_dt': log_dt, 'Lambda': Lambda, 'W': W, 'L': L_VAL}
    _L0_tok_all = _L0_tok_setup()
    _L0_tok_in = {k: v for k, v in _L0_tok_all.items() if k in ('log_dt', 'Lambda')}
    del _L0_tok_all

    def _L0_attn_setup():
        import jax, jax.numpy as jnp
        import numpy as np
        import math
        FACTOR = 1
        key = jax.random.key(seed)
        x = jax.random.normal(key, (8, 128, 1024), dtype=jnp.float32)
        return {'x': x}
    _L0_attn_all = _L0_attn_setup()
    _L0_attn_in = {k: v for k, v in _L0_attn_all.items() if k in ()}
    del _L0_attn_all

    def _L0_ffn_setup():
        import jax, jax.numpy as jnp
        import numpy as np
        import math
        B, S, IN, OUT = (4, 512, 1024, 1024)
        E, R, K = (8, 64, 128)
        SCALE = 64.0 / 64.0
        MULTIPLIER = 1.0
        key = jax.random.key(seed)
        ks = jax.random.split(key, 6)
        return {'x': jax.random.normal(ks[0], (B, S, IN), jnp.float32), 'W_org': jax.random.normal(ks[1], (OUT, IN), jnp.float32) * 0.02, 'lora_down': jax.random.normal(ks[2], (E, IN, R), jnp.float32) * 0.02, 'lora_up': jax.random.normal(ks[3], (E, R, OUT), jnp.float32) * 0.02, 'lora_keys': jax.random.normal(ks[4], (E, K), jnp.float32), 'Wq': jax.random.normal(ks[5], (K, IN), jnp.float32) * 0.02}
    _L0_ffn_all = _L0_ffn_setup()
    _L0_ffn_in = {k: v for k, v in _L0_ffn_all.items() if k in ('W_org', 'lora_down', 'lora_up', 'lora_keys', 'Wq')}
    del _L0_ffn_all
    return {'x': x, 'L0_tok_log_dt': _L0_tok_in['log_dt'], 'L0_tok_Lambda': _L0_tok_in['Lambda'], 'L0_ffn_W_org': _L0_ffn_in['W_org'], 'L0_ffn_lora_down': _L0_ffn_in['lora_down'], 'L0_ffn_lora_up': _L0_ffn_in['lora_up'], 'L0_ffn_lora_keys': _L0_ffn_in['lora_keys'], 'L0_ffn_Wq': _L0_ffn_in['Wq']}

def reference(x, L0_tok_log_dt, L0_tok_Lambda, L0_ffn_W_org, L0_ffn_lora_down, L0_ffn_lora_up, L0_ffn_lora_keys, L0_ffn_Wq):
    import jax
    import jax.numpy as jnp

    def _L0_tok_ref(log_dt, Lambda, W, L):
        import jax, jax.numpy as jnp
        import numpy as np
        import math
        H, N, C, L_VAL = (128, 64, 1, 1024)
        EPS = 1e-07

        def _reciprocal(x, epsilon):
            xc = jnp.conj(x)
            return xc / (x * xc + epsilon)
        Lam = Lambda[:, 0] + 1j * Lambda[:, 1]
        Wc = W[..., 0] + 1j * W[..., 1]
        dt = jnp.exp(log_dt)
        dt_Lambda = dt[:, None, 0] * Lambda[None, :, 0] + 1j * (dt[:, None, 1] * Lambda[None, :, 1])
        pos = jnp.arange(L, dtype=jnp.float32)
        gt0 = (Lam.real > 0).astype(dt_Lambda.real.dtype)
        P_max = jax.lax.stop_gradient(dt_Lambda * (gt0 * (L - 1)))
        dt_Lambda_neg = dt_Lambda * (1 - 2 * gt0)
        num = jnp.exp(dt_Lambda_neg) - 1
        den = jnp.exp(dt_Lambda_neg * L) - 1
        Wc = Wc * num * _reciprocal(den * Lam, EPS)
        P = dt_Lambda[..., None] * pos - P_max[..., None]
        K = jnp.einsum('chn,hnl->chl', Wc, jnp.exp(P))
        return K.real.astype(jnp.float32)

    def _L0_attn_ref(x):
        import jax, jax.numpy as jnp
        import numpy as np
        import math
        FACTOR = 1
        B, C, L = x.shape
        xh = x[:, None]
        f = jnp.fft.rfft(xh, axis=-1)
        corr = jnp.fft.irfft(f * jnp.conj(f), n=L, axis=-1)
        top_k = int(FACTOR * math.log(L))
        weights, delay = jax.lax.top_k(corr, top_k)
        tmp_corr = jax.nn.softmax(weights, axis=-1)
        init_index = jnp.arange(L)
        idx = (init_index[None, None, None, None, :] + delay[..., None]) % L
        pattern = jnp.take_along_axis(xh[:, :, :, None, :], idx, axis=-1)
        delays_agg = jnp.sum(pattern * tmp_corr[..., None], axis=-2)
        return delays_agg[:, 0]

    def _L0_ffn_ref(x, W_org, lora_down, lora_up, lora_keys, Wq):
        import jax, jax.numpy as jnp
        import numpy as np
        import math
        B, S, IN, OUT = (4, 512, 1024, 1024)
        E, R, K = (8, 64, 128)
        SCALE = 64.0 / 64.0
        MULTIPLIER = 1.0
        base = jnp.einsum('bsi,oi->bso', x, W_org)
        q = jnp.einsum('bi,ki->bk', x.mean(axis=1), Wq)
        scores = jnp.einsum('bk,ek->be', q, lora_keys) / math.sqrt(K)
        coeffs = jax.nn.softmax(scores, axis=-1)
        h = jnp.einsum('bsi,eir->bser', x, lora_down)
        delta = jnp.einsum('be,bser,ero->bso', coeffs, h, lora_up)
        return base + delta * (SCALE * MULTIPLIER)
    h = _L0_tok_ref(L0_tok_log_dt, L0_tok_Lambda, x, 1024)
    h = h + _L0_attn_ref(_layernorm(h, axis=-1))
    h = h + _L0_ffn_ref(_layernorm(h, axis=-1), L0_ffn_W_org, L0_ffn_lora_down, L0_ffn_lora_up, L0_ffn_lora_keys, L0_ffn_Wq)
    return h

_drawn_inputs = setup_inputs


def setup_inputs(seed=0):
    import zlib

    import numpy as np

    out = dict(_drawn_inputs(seed))
    spreads = {}
    factors = {'L0_ffn_lora_keys': 8.0, 'L0_ffn_Wq': 8.0}
    for name, (base, spread) in spreads.items():
        noise = np.random.default_rng([zlib.crc32(name.encode()), seed]).standard_normal(out[name].shape)
        drawn = base * np.exp(spread * noise) if base else spread * noise
        out[name] = jnp.asarray(drawn.astype(out[name].dtype))
    for name, factor in factors.items():
        out[name] = (out[name] * factor).astype(out[name].dtype)
    return out
```

```python
from contextlib import ExitStack

import numpy as np

import concourse.bass as bass
from concourse import mybir

F32 = mybir.dt.float32
F16 = mybir.dt.float16
U32 = mybir.dt.uint32
I32 = mybir.dt.int32
ALU = mybir.AluOpType
ACT = mybir.ActivationFunctionType
AX = mybir.AxisListType.X
RMAX = bass.bass_isa.ReduceOp.max

P = 128
NT = 64
H = 128
N = 64
L = 1024
HALF = L // 2
E, R, KEY = 8, 64, 128
ER = E * R
IC = L // P
RC = ER // P
Q = 256
M = 257
ROW = 2 * L
LN_EPS = 1e-5
REC_EPS = 1e-7
ROUND = 12582912.0
TURN = 6.283185
HB = 8
NB = H // HB
GATHERS = 5


def split16(a):
    hi = a.astype(np.float16)
    return hi, (a - hi.astype(np.float64)).astype(np.float16)


def dft_constants():
    w = 2 * np.pi / L
    l0, l1 = np.arange(Q)[:, None], np.arange(1, Q + 1)[:, None]
    even, odd = 2 * np.arange(Q)[None] + 2, 2 * np.arange(Q)[None] + 1
    re_even = np.cos(w * (l0 * even % L)) - np.cos(w * (Q * even % L))
    re_odd = np.cos(w * (l0 * odd % L))
    im_even = np.sin(w * (l1 * even % L))
    im_odd = np.sin(w * (l1 * odd % L))
    im_odd[-1] *= 0.5
    fwd = np.concatenate([re_even, re_odd, im_even, im_odd]).reshape(8, P, Q).transpose(1, 0, 2)
    m = np.arange(M)[None]
    weight = np.where(even.T == HALF, 1.0, 2.0)
    inv = np.concatenate([weight * np.cos(w * (even.T * m % L)), 2 * np.cos(w * (odd.T * m % L))])
    inv = inv.reshape(4, P, M).transpose(1, 0, 2)
    return np.stack(split16(fwd), 1), np.stack(split16(inv), 1)


def vit_tower(nc, wre, wim, log_dt, lam, w_org, down, up, keys, wq, fwd_c, inv_c, eye, out):
    with ExitStack() as ctx:
        def sb(name, shape, dt=F32):
            return ctx.enter_context(nc.sbuf_tensor(name, shape, dt))

        def sem(name):
            return ctx.enter_context(nc.semaphore(name))

        twice = nc.dram_tensor("k_twice", (NT * H * ROW, 1), F32, kind="Internal").ap()
        by_row = twice.rearrange("(r n) o -> r (n o)", n=ROW)
        by_half = twice.rearrange("(c h w a b) o -> w a c h (b o)", c=NT, h=H, w=2, a=2)
        out_rows = out.rearrange("c h l -> (c h) l")

        ident = sb("ident", [P, P])
        w16 = sb("w16", [P, 2, IC, L], F16)
        d16 = sb("d16", [P, 2, IC, ER], F16)
        kq16 = sb("kq16", [P, 2, IC, E], F16)
        fwd = sb("fwd", [P, 2, 8, Q], F16)
        inv = sb("inv", [P, 2, 4, M], F16)
        scale = sb("scale", [P, 8])
        zr = sb("zr", [P, H])
        turns = sb("turns", [P, H])
        s1 = sb("s1", [P, 2, H])
        s2 = sb("s2", [P, 2, H])
        pos = sb("pos", [P, HALF])
        side = sb("side", [P, 8])
        GROW, SIGN, LOWER, UPPER, NLOWER, PHASE, F0, F1 = range(8)

        tables(nc, locals())
        generate(nc, locals())
        tower(nc, locals())


def tables(nc, v):
    ident, w16, d16, kq16, fwd, inv, scale = (v[k] for k in ("ident", "w16", "d16", "kq16", "fwd", "inv", "scale"))
    zr, turns, s1, s2, pos, side = (v[k] for k in ("zr", "turns", "s1", "s2", "pos", "side"))
    w_org, down, up, keys, wq, log_dt, lam = (v[k] for k in ("w_org", "down", "up", "keys", "wq", "log_dt", "lam"))
    GROW, SIGN, LOWER, UPPER, NLOWER, PHASE, F0, F1 = range(8)
    with ExitStack() as ctx:
        def sb(name, shape, dt=F32):
            return ctx.enter_context(nc.sbuf_tensor(name, shape, dt))

        def sem(name):
            return ctx.enter_context(nc.semaphore(name))

        wf = sb("wf", [P, IC, L])
        df = sb("df", [P, IC, ER])
        uf = sb("uf", [P, RC, L])
        wqf = sb("wqf", [P, L])
        keysf = sb("keysf", [P, E])
        kqf = sb("kqf", [P, IC, E])
        peak = sb("peak", [P, 4])
        dip = sb("dip", [P, 4])
        top = sb("top", [P, 4])
        power = sb("power", [P, 4])
        rawscale = sb("rawscale", [P, 5])
        lamf = sb("lamf", [P, 2])
        dt = sb("dt", [P, 2, H])
        z = sb("z", [P, 2, H])
        zneg = sb("zneg", [P, 2, H])
        tin = sb("tin", [P, 2, H])
        th = sb("th", [P, 2, H])
        ein = sb("ein", [P, 2, H])
        ex = sb("ex", [P, 2, H])
        ang = sb("ang", [P, 8, H])
        whole = sb("whole", [P, 8, H])
        sn = sb("sn", [P, 8, H])
        wk = [sb(f"wk{i}", [P, 2, H]) for i in range(6)]
        re, im = sb("re", [P, 2, H]), sb("im", [P, 2, H])
        q = [sb(f"q{i}", [P, H]) for i in range(10)]
        ps_kq = ctx.enter_context(nc.psum_tensor("ps_kq", [P, IC * E], F32))

        loaded = sem("loaded")
        wq_loaded = sem("wq_loaded")
        kq_done = sem("kq_done")
        kq_copied = sem("kq_copied")
        peaks_ready = sem("peaks_ready")
        top_ready = sem("top_ready")
        scale_ready = sem("scale_ready")
        hi_ready = sem("hi_ready")
        small_loaded = sem("small_loaded")
        dt_ready = sem("dt_ready")
        args_ready = sem("args_ready")
        funcs_ready = sem("funcs_ready")
        pos_ready = sem("pos_ready")
        block = ctx.enter_context(nc.Block())

        @block.sync
        def _(sp):
            sp.dma_start(dt[:, 0, :], log_dt[0:1, :].partition_broadcast(P)).then_inc(small_loaded, 16)
            sp.dma_start(dt[:, 1, :], log_dt[1:2, :].partition_broadcast(P)).then_inc(small_loaded, 16)
            sp.dma_start(lamf[:, :], lam).then_inc(small_loaded, 16)
            sp.dma_start(wqf[:, :], wq).then_inc(wq_loaded, 16)
            sp.dma_start(keysf[:, :], keys).then_inc(wq_loaded, 16)
            sp.dma_start(wf[:, :, :], w_org.rearrange("(c p) o -> p c o", p=P)).then_inc(loaded, 16)
            sp.dma_start(df[:, :, :], down.rearrange("(c p) o -> p c o", p=P)).then_inc(loaded, 16)
            sp.dma_start(uf[:, :, :], up.rearrange("(c p) o -> p c o", p=P)).then_inc(loaded, 16)
            sp.dma_start(ident[:, :], v["eye"]).then_inc(loaded, 16)
            sp.dma_start(fwd[:, :, :, :], v["fwd_c"]).then_inc(loaded, 16)
            sp.dma_start(inv[:, :, :, :], v["inv_c"]).then_inc(loaded, 16)
            sp.wait_ge(loaded, 96)

        @block.tensor
        def _(pe):
            pe.wait_ge(wq_loaded, 32)
            for c in range(IC):
                last = nc.tensor.matmul(ps_kq[:, c * E:(c + 1) * E], wqf[:, c * P:(c + 1) * P], keysf[:, :],
                                        start=True, stop=True)
            last.then_inc(kq_done, 1)

        @block.gpsimd
        def _(pool):
            nc.gpsimd.iota(pos[:, :], [[1, HALF]], base=0, channel_multiplier=0,
                           allow_small_or_imprecise_dtypes=True).then_inc(pos_ready, 1)
            pool.wait_ge(peaks_ready, 1)
            nc.gpsimd.partition_all_reduce(top[:, :], peak[:, :], P, RMAX).then_inc(top_ready, 1)

        @block.scalar
        def _(act):
            act.wait_ge(small_loaded, 48)
            nc.scalar.activation(dt[:, :, :], dt[:, :, :], ACT.Exp).then_inc(dt_ready, 1)
            act.wait_ge(args_ready, 1)
            nc.scalar.activation(th[:, :, :], tin[:, :, :], ACT.Tanh).then_inc(funcs_ready, 1)
            nc.scalar.activation(ex[:, :, :], ein[:, :, :], ACT.Exp).then_inc(funcs_ready, 1)
            nc.scalar.activation(sn[:, :, :], ang[:, :, :], ACT.Sin, scale=TURN).then_inc(funcs_ready, 1)
            act.wait_ge(kq_done, 1)
            nc.scalar.activation(kqf[:, :, :], ps_kq[:, :].rearrange("p (c e) -> p c e", e=E), ACT.Copy)\
                .then_inc(kq_copied, 1)
            act.wait_ge(scale_ready, 1)
            nc.scalar.activation(w16[:, 0], wf[:, :, :], ACT.Copy, scale=scale[:, 0:1]).then_inc(hi_ready, 1)
            nc.scalar.activation(d16[:, 0], df[:, :, :], ACT.Copy, scale=scale[:, 1:2]).then_inc(hi_ready, 1)
            nc.scalar.activation(kq16[:, 0], kqf[:, :, :], ACT.Copy, scale=scale[:, 3:4]).then_inc(hi_ready, 1)

        @block.vector
        def _(dve):
            V = nc.vector

            def ts(out, in0, a, b=None, op0=ALU.mult, op1=ALU.bypass):
                V.tensor_scalar(out, in0, a, b, op0, op1)

            V.memset(side[:, :], 0.0)
            dve.drain()
            V.memset(side[0:N, LOWER:LOWER + 1], 1.0)
            V.memset(side[N:P, UPPER:UPPER + 1], 1.0)
            V.memset(side[0:N, NLOWER:NLOWER + 1], -1.0)
            V.memset(side[0:N, PHASE:PHASE + 1], 0.25)
            dve.wait_ge(small_loaded, 48)
            ts(side[:, GROW:GROW + 1], lamf[:, 0:1], 0.0, None, ALU.is_gt)
            dve.drain()
            ts(side[:, SIGN:SIGN + 1], side[:, GROW:GROW + 1], -2.0, 1.0, ALU.mult, ALU.add)
            ts(side[:, F0:F0 + 1], side[:, GROW:GROW + 1], -float(HALF))
            dve.wait_ge(pos_ready, 1)
            ts(power[:, 0:1], side[:, GROW:GROW + 1], -float(HALF - 1))
            dve.drain()
            ts(side[:, F1:F1 + 1], side[:, F0:F0 + 1], float(HALF), None, ALU.add)
            ts(pos[:, :], pos[:, :], power[:, 0:1], None, ALU.add)

            dve.wait_ge(dt_ready, 1)
            for k in range(2):
                ts(z[:, k], dt[:, k], lamf[:, k:k + 1])
            dve.drain()
            ts(zneg[:, :, :], z[:, :, :], side[:, SIGN:SIGN + 1])
            V.tensor_copy(zr[:, :], z[:, 0])
            ts(turns[:, :], z[:, 1], 1.0 / (2 * np.pi))
            dve.drain()
            for k, times in enumerate((1, L)):
                ts(tin[:, k], zneg[:, 0], 0.5 * times)
                ts(ang[:, 2 * k], zneg[:, 1], times / (4 * np.pi))
                ts(ang[:, 2 * k + 1], zneg[:, 1], times / (4 * np.pi), 0.25, ALU.mult, ALU.add)
            for a, col in enumerate((F0, F1)):
                f = side[:, col:col + 1]
                ts(ein[:, a], z[:, 0], f)
                ts(ang[:, 4 + 2 * a], turns[:, :], f)
                ts(ang[:, 5 + 2 * a], turns[:, :], f, 0.25, ALU.mult, ALU.add)
            dve.drain()
            ts(whole[:, :, :], ang[:, :, :], ROUND, -ROUND, ALU.add, ALU.add)
            dve.drain()
            V.tensor_tensor(ang[:, :, :], ang[:, :, :], whole[:, :, :], ALU.subtract)
            dve.drain().then_inc(args_ready, 1)

            dve.wait_ge(funcs_ready, 3)
            sin_half, cos_half = sn[:, 0:4:2], sn[:, 1:4:2]
            ts(wk[0][:, :, :], th[:, :, :], -1.0, 1.0, ALU.mult, ALU.add)
            V.scalar_tensor_tensor(wk[2][:, :, :], sin_half, -2.0, sin_half, ALU.mult, ALU.mult)
            V.scalar_tensor_tensor(wk[3][:, :, :], sin_half, 2.0, cos_half, ALU.mult, ALU.mult)
            dve.drain()
            V.reciprocal(wk[1][:, :, :], wk[0][:, :, :])
            dve.drain()
            V.scalar_tensor_tensor(wk[4][:, :, :], th[:, :, :], 2.0, wk[1][:, :, :], ALU.mult, ALU.mult)
            dve.drain()
            V.scalar_tensor_tensor(wk[5][:, :, :], wk[2][:, :, :], 1.0, wk[4][:, :, :], ALU.add, ALU.mult)
            V.scalar_tensor_tensor(im[:, :, :], wk[4][:, :, :], 1.0, wk[3][:, :, :], ALU.add, ALU.mult)
            dve.drain()
            V.tensor_tensor(re[:, :, :], wk[5][:, :, :], wk[2][:, :, :], ALU.add)
            dve.drain()
            lr, li = lamf[:, 0:1], lamf[:, 1:2]
            ts(q[0][:, :], im[:, 1], li)
            ts(q[1][:, :], im[:, 1], lr)
            dve.drain()
            V.scalar_tensor_tensor(q[2][:, :], re[:, 1], lr, q[0][:, :], ALU.mult, ALU.subtract)
            V.scalar_tensor_tensor(q[3][:, :], re[:, 1], li, q[1][:, :], ALU.mult, ALU.add)
            dve.drain()
            V.tensor_tensor(q[4][:, :], q[2][:, :], q[2][:, :], ALU.mult)
            V.tensor_tensor(q[5][:, :], q[3][:, :], q[3][:, :], ALU.mult)
            V.tensor_tensor(q[6][:, :], re[:, 0], q[2][:, :], ALU.mult)
            V.tensor_tensor(q[7][:, :], im[:, 0], q[3][:, :], ALU.mult)
            V.tensor_tensor(q[8][:, :], im[:, 0], q[2][:, :], ALU.mult)
            V.tensor_tensor(q[9][:, :], re[:, 0], q[3][:, :], ALU.mult)
            dve.drain()
            V.scalar_tensor_tensor(q[0][:, :], q[4][:, :], REC_EPS, q[5][:, :], ALU.add, ALU.add)
            dve.drain()
            V.reciprocal(q[1][:, :], q[0][:, :])
            V.tensor_tensor(q[2][:, :], q[6][:, :], q[7][:, :], ALU.add)
            V.tensor_tensor(q[3][:, :], q[8][:, :], q[9][:, :], ALU.subtract)
            dve.drain()
            V.tensor_tensor(q[4][:, :], q[2][:, :], q[1][:, :], ALU.mult)
            V.tensor_tensor(q[5][:, :], q[3][:, :], q[1][:, :], ALU.mult)
            V.tensor_tensor(wk[0][:, :, :], ex[:, :, :], sn[:, 5:8:2], ALU.mult)
            V.tensor_tensor(wk[1][:, :, :], ex[:, :, :], sn[:, 4:8:2], ALU.mult)
            dve.drain()
            for a in range(2):
                V.tensor_tensor(q[6][:, :], q[4][:, :], wk[0][:, a], ALU.mult)
                V.tensor_tensor(q[7][:, :], q[5][:, :], wk[1][:, a], ALU.mult)
                V.tensor_tensor(q[8][:, :], q[4][:, :], wk[1][:, a], ALU.mult)
                V.tensor_tensor(q[9][:, :], q[5][:, :], wk[0][:, a], ALU.mult)
                dve.drain()
                V.tensor_tensor(q[0][:, :], q[6][:, :], q[7][:, :], ALU.subtract)
                V.tensor_tensor(q[1][:, :], q[8][:, :], q[9][:, :], ALU.add)
                dve.drain()
                ts(q[2][:, :], q[1][:, :], side[:, UPPER:UPPER + 1])
                ts(q[3][:, :], q[0][:, :], side[:, UPPER:UPPER + 1])
                dve.drain()
                V.scalar_tensor_tensor(s1[:, a], q[0][:, :], side[:, LOWER:LOWER + 1], q[2][:, :], ALU.mult, ALU.subtract)
                V.scalar_tensor_tensor(s2[:, a], q[1][:, :], side[:, NLOWER:NLOWER + 1], q[3][:, :], ALU.mult, ALU.subtract)
                dve.drain()

            dve.wait_ge(loaded, 96)
            dve.wait_ge(kq_copied, 1)
            for k, t in enumerate((wf, df, uf, kqf)):
                flat = t[:, :, :].rearrange("p a b -> p (a b)")
                V.tensor_reduce(peak[:, k:k + 1], flat, axis=AX, op=ALU.max)
                V.tensor_reduce(dip[:, k:k + 1], flat, axis=AX, op=ALU.min)
            dve.drain()
            V.scalar_tensor_tensor(peak[:, :], dip[:, :], -1.0, peak[:, :], ALU.mult, ALU.max)
            dve.drain().then_inc(peaks_ready, 1)
            dve.wait_ge(top_ready, 1)
            V.tensor_scalar(power[:, :].bitcast(I32), top[:, :].bitcast(I32), 0x7F800000, None, ALU.bitwise_and)
            dve.drain()
            ts(power[:, :], power[:, :], 2.0 ** -60, None, ALU.max)
            dve.drain()
            V.reciprocal(rawscale[:, 0:4], power[:, :])
            dve.drain()
            V.tensor_copy(scale[:, 1:2], rawscale[:, 1:2])
            V.tensor_copy(scale[:, 3:4], rawscale[:, 3:4])
            V.tensor_tensor(rawscale[:, 4:5], rawscale[:, 1:2], rawscale[:, 2:3], ALU.mult)
            ts(scale[:, 5:6], power[:, 3:4], 1.0 / np.sqrt(KEY))
            dve.drain()
            V.tensor_tensor(scale[:, 0:1], rawscale[:, 0:1], rawscale[:, 4:5], ALU.min)
            dve.drain()
            V.tensor_tensor(scale[:, 2:3], scale[:, 0:1], power[:, 1:2], ALU.mult)
            V.reciprocal(scale[:, 4:5], scale[:, 0:1])
            dve.drain().then_inc(scale_ready, 1)
            for k, (t, t16) in enumerate(((wf, w16), (df, d16), (kqf, kq16))):
                dve.wait_ge(hi_ready, k + 1)
                col = (0, 1, 3)[k]
                V.scalar_tensor_tensor(t16[:, 1], t[:, :, :], scale[:, col:col + 1], t16[:, 0], ALU.mult, ALU.subtract)


def generate(nc, v):
    zr, turns, s1, s2, pos, side = (v[k] for k in ("zr", "turns", "s1", "s2", "pos", "side"))
    wre, wim, by_half = v["wre"], v["wim"], v["by_half"]
    PHASE = 5
    with ExitStack() as ctx:
        def sb(name, shape, dt=F32):
            return ctx.enter_context(nc.sbuf_tensor(name, shape, dt))

        def sem(name):
            return ctx.enter_context(nc.semaphore(name))

        wa = sb("wa", [P, 2, HB, N])
        wb = sb("wb", [P, 2, HB, N])
        pr = sb("pr", [P, HB, N])
        wp = sb("wp", [P, 2, HB, 2, N])
        zrb = sb("zrb", [P, 2, HB])
        tub = sb("tub", [P, 2, HB])
        ang = sb("angle", [P, 2, HB, HALF])
        whole = sb("whole_turns", [P, HB, HALF])
        amp = sb("amp", [P, 2, HB, HALF])
        HG = HB // 2
        kst = sb("kst", [P, 2, HG, HALF])
        ps = ctx.enter_context(nc.psum_tensor("ps_k", [P, HB, HALF], F32))

        w_loaded = [sem(f"w_loaded{u}") for u in range(2)]
        w_used = sem("w_used")
        par_ready = sem("par_ready")
        exp_done = sem("exp_done")
        whole_ready = sem("whole_ready")
        part_ready = sem("part_ready")
        sin_done = sem("sin_done")
        wave_ready = sem("wave_ready")
        wp_ready = sem("wp_ready")
        k_done = sem("k_done")
        copied_act = sem("copied_act")
        copied_dve = sem("copied_dve")
        stored = [sem(f"stored{g}") for g in range(2)]
        block = ctx.enter_context(nc.Block())

        def blocks(eng, body):
            body(0, 0)
            body(0, 1)
            with eng.Fori(1, NB // 2) as r:
                body(r, 0)
                body(r, 1)

        def upto(eng, sm, r, u, off, per=1):
            if isinstance(r, int):
                if 2 * r + u + off >= 0:
                    eng.wait_ge(sm, per * (2 * r + u + off + 1))
            else:
                eng.wait_ge(sm, r * (2 * per) + per * (u + off + 1))

        @block.sync
        def _(sp):
            def body(r, u):
                h0 = (2 * r + u) * HB if isinstance(r, int) else sp.snap(r * (2 * HB) + u * HB)
                need = None if isinstance(r, int) else sp.snap(r * 2 + (u - 1))
                stored_before = None if isinstance(r, int) else sp.snap(r * 64 + 32 * u)
                cp = None if isinstance(r, int) else sp.snap(r * (2 * HG) + HG * u)
                if need is not None:
                    sp.wait_ge(w_used, need)
                sp.dma_start(wa[:, u], wre[:, bass.ds(h0, HB), :]).then_inc(w_loaded[u], 16)
                sp.dma_start(wb[:, u], wim[:, bass.ds(h0, HB), :]).then_inc(w_loaded[u], 16)

            body(0, 0)
            body(0, 1)

            def store(r, u, load):
                static = isinstance(r, int)
                b = 2 * r + u if static else None
                h0 = b * HB if static else sp.snap(r * (2 * HB) + u * HB)
                h1 = b * HB + HG if static else sp.snap(r * (2 * HB) + u * HB + HG)
                n = HG * (b + 1) if static else sp.snap(r * (2 * HG) + HG * (u + 1))
                for g, (copied, hh) in enumerate(((copied_act, h0), (copied_dve, h1))):
                    for w in range(2):
                        for a in range(2):
                            sp.wait_ge(copied, n)
                            sp.dma_start(by_half[w, a, :, bass.ds(hh, HG), :],
                                         kst[a * N:(a + 1) * N, g]).then_inc(stored[g], 16)
                if load:
                    body2(r, u)

            def body2(r, u):
                static = isinstance(r, int)
                h2 = (2 * r + u + 2) * HB if static else sp.snap(r * (2 * HB) + (u + 2) * HB)
                need = 2 * r + u + 1 if static else sp.snap(r * 2 + (u + 1))
                for w_s, src in ((wa, wre), (wb, wim)):
                    sp.wait_ge(w_used, need)
                    sp.dma_start(w_s[:, u], src[:, bass.ds(h2, HB), :]).then_inc(w_loaded[u], 16)

            with sp.Fori(0, NB // 2 - 1) as r:
                store(r, 0, True)
                store(r, 1, True)
            store(NB // 2 - 1, 0, False)
            store(NB // 2 - 1, 1, False)
            for g in range(2):
                sp.wait_ge(stored[g], 64 * NB)

        @block.gpsimd
        def _(pool):
            def body(r, u):
                upto(pool, whole_ready, r, u, 0)
                nc.gpsimd.tensor_tensor(ang[:, u], ang[:, u], whole[:, :, :], ALU.subtract).then_inc(part_ready, 1)
            blocks(pool, body)

        @block.scalar
        def _(act):
            def copies(r, u, off):
                for j in range(HG):
                    upto(act, k_done, r, u, off)
                    if j == 0:
                        upto(act, stored[0], r, u, off - 1, 64)
                    nc.scalar.activation(kst[:, 0, j], ps[:, j], ACT.Copy).then_inc(copied_act, 1)

            def body(r, u):
                upto(act, par_ready, r, u, 0)
                for j in range(HB):
                    if j == 0:
                        upto(act, k_done, r, u, -2)
                    last = nc.scalar.activation(amp[:, u, j], pos[:, :], ACT.Exp, scale=zrb[:, u, j:j + 1])
                last.then_inc(exp_done, 1)
                if not isinstance(r, int) or 2 * r + u >= 1:
                    copies(r, u, -1)
                upto(act, part_ready, r, u, 0)
                nc.scalar.activation(ang[:, u], ang[:, u], ACT.Sin, scale=TURN).then_inc(sin_done, 1)
            blocks(act, body)
            copies(NB // 2, 0, -1)

        @block.vector
        def _(dve):
            V = nc.vector

            def angles(r, u):
                cols = slice((2 * r + u) * HB, (2 * r + u + 1) * HB) if isinstance(r, int) \
                    else bass.ds(r * (2 * HB) + u * HB, HB)
                upto(dve, exp_done, r, u, -2)
                V.tensor_copy(zrb[:, u], zr[:, cols])
                V.tensor_copy(tub[:, u], turns[:, cols])
                dve.drain().then_inc(par_ready, 1)
                for j in range(HB):
                    V.tensor_scalar(ang[:, u, j], pos[:, :], tub[:, u, j:j + 1], side[:, PHASE:PHASE + 1],
                                    ALU.mult, ALU.add)
                dve.drain()
                upto(dve, part_ready, r, u, -1)
                V.tensor_scalar(whole[:, :, :], ang[:, u], ROUND, -ROUND, ALU.add, ALU.add).then_inc(whole_ready, 1)

            def stationary(r, u):
                cols = slice((2 * r + u) * HB, (2 * r + u + 1) * HB) if isinstance(r, int) \
                    else bass.ds(r * (2 * HB) + u * HB, HB)
                if isinstance(r, int):
                    dve.wait_ge(w_loaded[u], 32 * (r + 1))
                else:
                    dve.wait_ge(w_loaded[u], r * 32 + 32)
                for a in range(2):
                    m1 = s1[:, a, cols].unsqueeze(2).broadcast_to([P, HB, N])
                    m2 = s2[:, a, cols].unsqueeze(2).broadcast_to([P, HB, N])
                    V.tensor_tensor(pr[:, :, :], wb[:, u], m2, ALU.mult)
                    if a == 0:
                        upto(dve, k_done, r, u, -2)
                    V.tensor_tensor(wp[:, u, :, a], wa[:, u], m1, ALU.mult)
                    dve.drain()
                    V.tensor_tensor(wp[:, u, :, a], wp[:, u, :, a], pr[:, :, :], ALU.add)
                    dve.drain()
                dve.drain().then_inc(w_used, 1)

            def wave(r, u, off):
                w = (u + off) % 2
                upto(dve, sin_done, r, u, off)
                upto(dve, exp_done, r, u, off)
                V.tensor_tensor(amp[:, w], amp[:, w], ang[:, w], ALU.mult).then_inc(wave_ready, 1)

            def copies(r, u, off):
                for j in range(HG):
                    upto(dve, k_done, r, u, off)
                    if j == 0:
                        upto(dve, stored[1], r, u, off - 1, 64)
                    V.tensor_copy(kst[:, 1, j], ps[:, HG + j]).then_inc(copied_dve, 1)

            def body(r, u):
                angles(r, u)
                stationary(r, u)
                if not isinstance(r, int) or 2 * r + u >= 1:
                    copies(r, u, -1)
                wave(r, u, 0)
            blocks(dve, body)
            copies(NB // 2, 0, -1)

        @block.tensor
        def _(pe):
            def body(r, u):
                upto(pe, w_used, r, u, 0)
                upto(pe, wave_ready, r, u, 0)
                upto(pe, copied_act, r, u, -1, HG)
                upto(pe, copied_dve, r, u, -1, HG)
                for j in range(HB):
                    last = nc.tensor.matmul(ps[:, j], wp[:, u, j].rearrange("p a c -> p (a c)"), amp[:, u, j],
                                            start=True, stop=True)
                last.then_inc(k_done, 1)
            blocks(pe, body)


def tower(nc, v):
    ident, w16, d16, kq16, fwd, inv, scale = (v[k] for k in ("ident", "w16", "d16", "kq16", "fwd", "inv", "scale"))
    twice, by_row, out_rows, up = v["twice"], v["by_row"], v["out_rows"], v["up"]
    with ExitStack() as ctx:
        def sb(name, shape, dt=F32):
            return ctx.enter_context(nc.sbuf_tensor(name, shape, dt))

        def sem(name):
            return ctx.enter_context(nc.semaphore(name))

        u16 = sb("u16", [P, 2, RC, L], F16)
        kt = sb("kt", [P, 2, L])
        xn = sb("xn", [P, L])
        evn = sb("evn", [P, HALF + 1])
        odd = sb("odd", [P, HALF])
        fo = sb("fo", [P, 2, 4, Q])
        foT = sb("foT", [P, 2, 8, P], F16)
        sq = sb("sq", [P, 2, HALF])
        pw = sb("pw", [P, HALF])
        pT = sb("pT", [P, 2, 4, P], F16)
        osb = sb("osb", [P, M])
        cb = sb("cb", [P, HALF + 1])
        gb = sb("gb", [P, GATHERS, L])
        x2 = sb("x2", [P, 2, L])
        x2n = sb("x2n", [P, L])
        xT = sb("xT", [P, 2, 2, IC, P], F16)
        hs = sb("hs", [P, ER])
        hT = sb("hT", [P, 2, RC, P], F16)
        mean_of = sb("mean_of", [P, P])
        sc = sb("sc", [P, E])
        ex8 = sb("ex8", [P, E])
        soft = sb("soft", [P, 4])
        st = sb("st", [P, 12])
        mv = sb("mv", [P, 2])
        st2 = sb("st2", [P, 12])
        mv2 = sb("mv2", [P, 2])
        c1 = sb("c1", [P, 2, 2])
        n1 = sb("n1", [P, 2, 2])
        c2 = sb("c2", [P, 2])
        n2 = sb("n2", [P, 2])
        mhalf = sb("mhalf", [P, 1])
        m8 = sb("m8", [P, 8])
        i8 = sb("i8", [P, 8], U32)
        lag = sb("lag", [P, GATHERS], U32)
        mir = sb("mir", [P, 3])
        own = sb("own", [P, 2])
        notown = sb("notown", [P, 2])
        keep = sb("keep", [P, 4])
        idx = sb("idx", [P, GATHERS], U32)
        rowbase = sb("rowbase", [P, 1], U32)
        rowstep = sb("rowstep", [P, 1], U32)
        val = sb("val", [P, 6])
        nv0 = sb("nv0", [P, 1])
        e6 = sb("e6", [P, 6])
        wsum = sb("wsum", [P, 1])
        rsum = sb("rsum", [P, 2])
        wf = sb("wfac", [P, 2, 8])

        tr = ctx.enter_context(nc.psum_tensor("tr", [P, 2, 512], F32))
        fe = ctx.enter_context(nc.psum_tensor("fe", [P, 2, 512], F32))
        acc = ctx.enter_context(nc.psum_tensor("acc", [P, 2, 512], F32))
        hps = ctx.enter_context(nc.psum_tensor("hps", [P, 512], F32))
        small = ctx.enter_context(nc.psum_tensor("small", [P, 512], F32))

        k_loaded = [sem(f"k_loaded{u}") for u in range(2)]
        base_loaded = [sem(f"base_loaded{u}") for u in range(2)]
        out_stored = [sem(f"out_stored{u}") for u in range(2)]
        up_loaded, up_hi, up_lo = sem("up_loaded"), sem("up_hi"), sem("up_lo")
        const_ready = sem("const_ready")
        base_ready = sem("base_ready")
        names = ("stats1 rstd1 norm1 xn_ready fold_even even_folded fold_odd1 fold_odd t1_done foT_hi foT_lo f_done sq_done "
                 "p_ready t2_done pT_hi pT_lo i_done o_copied corr_done vals_ready wexp_done "
                 "wf_ready acc0_done x2_ready stats2 rstd2 norm2 x2n_ready t3_done xT_hi xT_lo ds_done s_copied "
                 "mean_done smax_done sexp_done hs_ready h_tr hT_hi hT_lo base_done acc_done out_ready").split()
        S = {n: sem(n) for n in names}
        gathered = sem("gathered")
        block = ctx.enter_context(nc.Block())

        FIRST, LOOP = -3, (1, 30)

        def steps(eng, step):
            for i in range(FIRST, 2 * LOOP[0]):
                step(i // 2, i % 2)
            with eng.Fori(LOOP[0], LOOP[1]) as r:
                step(r, 0)
                step(r, 1)
            for i in range(2 * LOOP[1], NT + 1):
                step(i // 2, i % 2)

        def has(r, u, off):
            return not isinstance(r, int) or 0 <= 2 * r + u + off < NT

        def upto(eng, name, r, u, off, per=1):
            sm = S[name]
            if isinstance(r, int):
                if 2 * r + u + off >= 0:
                    eng.wait_ge(sm, per * (2 * r + u + off + 1))
            else:
                eng.wait_ge(sm, r * (2 * per) + per * (u + off + 1))

        def dma_upto(eng, sems, r, u, off):
            p, k = (u + off) % 2, (u + off) // 2
            if isinstance(r, int):
                if r + k >= 0:
                    eng.wait_ge(sems[p], 16 * (r + k + 1))
            else:
                eng.wait_ge(sems[p], r * 16 + 16 * (k + 1))

        @block.sync
        def _(sp):
            sp.dma_start(gb[:, 0:RC, :], up.rearrange("(c p) o -> p c o", p=P)).then_inc(up_loaded, 16)

            def number(r, mult, add):
                return mult * r + add if isinstance(r, int) else sp.snap(r * mult + add)

            def step(r, u):
                t4, t1, tm = ((u + o) % 2 for o in (4, 1, -1))
                row4, row1, rowm = (number(r, 2 * H, (u + o) * H) for o in (4, 1, -1))
                xn_need = number(r, 2, u + 3)
                out_need = number(r, 2, u)
                st_need = number(r, 16, 16 * ((u - 1) // 2 + 1))
                if has(r, u, 4):
                    if not isinstance(r, int) or 2 * r + u + 2 >= 0:
                        sp.wait_ge(S["xn_ready"], xn_need)
                    sp.dma_start(kt[:, t4], by_row[bass.ds(row4, H), 0:L]).then_inc(k_loaded[t4], 16)
                if has(r, u, -1):
                    sp.wait_ge(S["out_ready"], out_need)
                    sp.dma_start(out_rows[bass.ds(rowm, H), :], x2[:, tm]).then_inc(out_stored[tm], 16)
                if has(r, u, 1):
                    if has(r, u, -1):
                        sp.wait_ge(out_stored[tm], st_need)
                    sp.dma_start(x2[:, t1], by_row[bass.ds(row1, H), 0:L]).then_inc(base_loaded[t1], 16)

            sp.dma_start(kt[:, 0], by_row[0:H, 0:L]).then_inc(k_loaded[0], 16)
            steps(sp, step)
            for u in range(2):
                sp.wait_ge(out_stored[u], 16 * NT // 2)

        @block.gpsimd
        def _(pool):
            G = nc.gpsimd
            G.memset(mean_of[:, :], 1.0 / H).then_inc(const_ready, 1)
            G.memset(mhalf[:, :], -0.5).then_inc(const_ready, 1)
            G.iota(rowbase[:, :], [[0, 1]], base=0, channel_multiplier=ROW).then_inc(const_ready, 1)
            G.memset(rowstep[:, :], H * ROW).then_inc(const_ready, 1)
            pool.wait_ge(const_ready, 4)
            pool.wait_ge(up_lo, 1)

            def step(r, u):
                if has(r, u, 3):
                    a = (u + 3) % 2
                    upto(pool, "stats1", r, u, 3)
                    G.tensor_tensor(n1[:, a, 0:1], c1[:, a, 0:1], mhalf[:, :], ALU.pow).then_inc(S["rstd1"], 1)
                    upto(pool, "rstd1", r, u, 3)
                    G.tensor_tensor(n1[:, a, 1:2], c1[:, a, 1:2], n1[:, a, 0:1], ALU.mult).then_inc(S["norm1"], 1)
                    upto(pool, "xn_ready", r, u, 3)
                    G.tensor_tensor(odd[:, 1:HALF], xn[:, 1:HALF], xn[:, L - 1:HALF:-1], ALU.subtract)\
                        .then_inc(S["fold_odd1"], 1)
                    upto(pool, "fold_odd1", r, u, 3)
                    upto(pool, "t1_done", r, u, 1)
                    lo, hi = odd[:, 1:Q + 1], odd[:, HALF - 1:Q - 1:-1]
                    G.tensor_tensor(fo[:, a, 2], lo, hi, ALU.subtract).then_inc(S["fold_odd"], 1)
                    G.tensor_tensor(fo[:, a, 3], lo, hi, ALU.add).then_inc(S["fold_odd"], 1)
                if has(r, u, 2):
                    upto(pool, "t2_done", r, u, 1)
                    upto(pool, "sq_done", r, u, 2)
                    G.tensor_tensor(pw[:, :], sq[:, 0], sq[:, 1], ALU.add).then_inc(S["p_ready"], 1)
                if has(r, u, 1):
                    upto(pool, "stats2", r, u, 1)
                    G.tensor_tensor(n2[:, 0:1], c2[:, 0:1], mhalf[:, :], ALU.pow).then_inc(S["rstd2"], 1)
                    upto(pool, "rstd2", r, u, 1)
                    G.tensor_tensor(n2[:, 1:2], c2[:, 1:2], n2[:, 0:1], ALU.mult).then_inc(S["norm2"], 1)
                if has(r, u, 2):
                    upto(pool, "x2_ready", r, u, 1)
                    upto(pool, "vals_ready", r, u, 2)
                    G.tensor_tensor(idx[:, :], lag[:, :], rowbase[:, :].broadcast_to([P, GATHERS]), ALU.add)
                    pool.drain()
                    G.tensor_tensor(rowbase[:, :], rowbase[:, :], rowstep[:, :], ALU.add)
                    for s in range(GATHERS):
                        G.indirect_dma_start(gb[:, s], None, twice,
                                             bass.IndirectOffsetOnAxis(ap=idx[:, s:s + 1], axis=0)).then_inc(gathered, 16)
            steps(pool, step)

        @block.scalar
        def _(act):
            A = nc.scalar.activation
            act.wait_ge(up_loaded, 16)
            A(u16[:, 0], gb[:, 0:RC, :], ACT.Copy, scale=scale[:, 2:3]).then_inc(up_hi, 1)

            def step(r, u):
                if has(r, u, 3):
                    a = (u + 3) % 2
                    upto(act, "norm1", r, u, 3)
                    upto(act, "fold_even", r, u, 2)
                    upto(act, "fold_odd1", r, u, 2)
                    A(xn[:, :], kt[:, a], ACT.Identity, scale=n1[:, a, 0:1], bias=n1[:, a, 1:2]).then_inc(S["xn_ready"], 1)
                if has(r, u, 0):
                    upto(act, "ds_done", r, u, 0)
                    A(sc[:, :], small[:, 0:E], ACT.Copy).then_inc(S["s_copied"], 1)
                if has(r, u, 2):
                    upto(act, "f_done", r, u, 1)
                    upto(act, "t1_done", r, u, 2)
                    A(foT[:, 0].rearrange("p c h -> p (c h)"), tr[:, :, :].rearrange("p a b -> p (a b)"), ACT.Copy)\
                        .then_inc(S["foT_hi"], 1)
                if has(r, u, 0):
                    upto(act, "smax_done", r, u, 0)
                    A(ex8[:, :], small[:, E:2 * E], ACT.Exp, scale=scale[:, 5:6], bias=soft[:, 1:2],
                      accum_out=soft[:, 2:3]).then_inc(S["sexp_done"], 1)
                if has(r, u, 1):
                    t = (u + 1) % 2
                    upto(act, "wf_ready", r, u, 1)
                    dma_upto(act, base_loaded, r, u, 1)
                    A(x2[:, t], x2[:, t], ACT.Identity, scale=wf[:, t, 6:7], bias=wf[:, t, 7:8])\
                        .then_inc(S["acc0_done"], 1)
                if has(r, u, 2):
                    upto(act, "p_ready", r, u, 1)
                    upto(act, "f_done", r, u, 2)
                    A(sq[:, :, :], fe[:, :, :], ACT.Square, scale=1.0 / 32).then_inc(S["sq_done"], 1)
                if has(r, u, 0):
                    upto(act, "acc_done", r, u, -1)
                    upto(act, "h_tr", r, u, 0)
                    A(hT[:, 0].rearrange("p c h -> p (c h)"), tr[:, 1], ACT.Copy).then_inc(S["hT_hi"], 1)
                if has(r, u, 2):
                    upto(act, "i_done", r, u, 1)
                    upto(act, "t2_done", r, u, 2)
                    A(pT[:, 0].rearrange("p c h -> p (c h)"), tr[:, 0], ACT.Copy).then_inc(S["pT_hi"], 1)
                if has(r, u, 1):
                    upto(act, "norm2", r, u, 1)
                    upto(act, "t3_done", r, u, 0)
                    t = (u + 1) % 2
                    A(x2n[:, :], x2[:, t], ACT.Identity, scale=n2[:, 0:1], bias=n2[:, 1:2]).then_inc(S["x2n_ready"], 1)
                if has(r, u, 2):
                    upto(act, "corr_done", r, u, 1)
                    upto(act, "i_done", r, u, 2)
                    A(osb[:, :], fe[:, 1, 0:M], ACT.Copy).then_inc(S["o_copied"], 1)
                if has(r, u, 1):
                    t = (u + 1) % 2
                    upto(act, "base_done", r, u, -1)
                    upto(act, "t3_done", r, u, 1)
                    A(xT[:, t, 0].rearrange("p c h -> p (c h)"), tr[:, :, :].rearrange("p a b -> p (a b)"), ACT.Copy)\
                        .then_inc(S["xT_hi"], 1)
                if has(r, u, 2):
                    upto(act, "vals_ready", r, u, 2)
                    A(e6[:, :], val[:, :], ACT.Exp, bias=nv0[:, :], accum_out=wsum[:, :]).then_inc(S["wexp_done"], 1)
            steps(act, step)

        @block.vector
        def _(dve):
            V = nc.vector

            def ts(out, in0, a, b=None, op0=ALU.mult, op1=ALU.bypass):
                return V.tensor_scalar(out, in0, a, b, op0, op1)

            stt = V.scalar_tensor_tensor
            dve.wait_ge(up_hi, 1)
            stt(u16[:, 1], gb[:, 0:RC, :], scale[:, 2:3], u16[:, 0], ALU.mult, ALU.subtract).then_inc(up_lo, 1)
            dve.wait_ge(const_ready, 4)

            def stats(src, st_, mv_, c_, name):
                V.bn_stats(st_[:, 0:6], src[:, 0:512])
                V.bn_stats(st_[:, 6:12], src[:, 512:1024])
                dve.drain()
                V.bn_aggr(mv_[:, :], st_[:, :])
                dve.drain()
                ts(c_[:, 0:1], mv_[:, 1:2], LN_EPS, None, ALU.add)
                ts(c_[:, 1:2], mv_[:, 0:1], -1.0)
                dve.drain().then_inc(S[name], 1)

            def step(r, u):
                if has(r, u, -1):
                    upto(dve, "acc_done", r, u, -1)
                    t = (u - 1) % 2
                    stt(x2[:, t], acc[:, :, :].rearrange("p a b -> p (a b)"), scale[:, 4:5], x2[:, t],
                        ALU.mult, ALU.add).then_inc(S["out_ready"], 1)
                if has(r, u, 1):
                    t = (u + 1) % 2
                    upto(dve, "wexp_done", r, u, 1)
                    V.reciprocal(rsum[:, 0:1], wsum[:, :])
                    dve.drain()
                    V.tensor_tensor(rsum[:, 1:2], rsum[:, 0:1], n1[:, t, 0:1], ALU.mult)
                    dve.drain()
                    ts(wf[:, t, 0:6], e6[:, :], rsum[:, 1:2])
                    ts(wf[:, t, 6:7], e6[:, 5:6], rsum[:, 1:2], 1.0, ALU.mult, ALU.add)
                    V.tensor_copy(wf[:, t, 7:8], n1[:, t, 1:2])
                    dve.drain().then_inc(S["wf_ready"], 1)
                if has(r, u, 3):
                    a = (u + 3) % 2
                    dma_upto(dve, k_loaded, r, u, 3)
                    stats(kt[:, a], st, mv, c1[:, a], "stats1")
                if has(r, u, 0):
                    upto(dve, "mean_done", r, u, 0)
                    V.tensor_reduce(soft[:, 0:1], small[:, E:2 * E], axis=AX, op=ALU.max)
                    dve.drain()
                    ts(soft[:, 1:2], soft[:, 0:1], scale[:, 5:6], -1.0, ALU.mult, ALU.mult).then_inc(S["smax_done"], 1)
                if has(r, u, 2):
                    upto(dve, "foT_hi", r, u, 2)
                    V.tensor_tensor(foT[:, 1].rearrange("p c h -> p (c h)"), tr[:, :, :].rearrange("p a b -> p (a b)"),
                                    foT[:, 0].rearrange("p c h -> p (c h)"), ALU.subtract).then_inc(S["foT_lo"], 1)
                if has(r, u, 0):
                    upto(dve, "sexp_done", r, u, 0)
                    V.reciprocal(soft[:, 3:4], soft[:, 2:3])
                    dve.drain()
                    upto(dve, "h_tr", r, u, -1)
                    stt(hs[:, :].rearrange("p (e r) -> p e r", e=E), hps[:, :].rearrange("p (e r) -> p e r", e=E),
                        soft[:, 3:4], ex8[:, :].unsqueeze(2).broadcast_to([P, E, R]), ALU.mult, ALU.mult)\
                        .then_inc(S["hs_ready"], 1)
                if has(r, u, 3):
                    a = (u + 3) % 2
                    upto(dve, "xn_ready", r, u, 3)
                    V.tensor_tensor(evn[:, 1:HALF], xn[:, 1:HALF], xn[:, L - 1:HALF:-1], ALU.add)
                    V.tensor_copy(evn[:, 0:HALF + 1:HALF], xn[:, 0:HALF + 1:HALF])
                    dve.drain().then_inc(S["fold_even"], 1)
                    upto(dve, "t1_done", r, u, 1)
                    lo, hi = evn[:, 0:Q], evn[:, HALF:Q:-1]
                    V.tensor_tensor(fo[:, a, 0], lo, hi, ALU.add)
                    V.tensor_tensor(fo[:, a, 1], lo, hi, ALU.subtract)
                    dve.drain().then_inc(S["even_folded"], 1)
                if has(r, u, 1):
                    t = (u + 1) % 2
                    upto(dve, "acc0_done", r, u, 1)
                    if isinstance(r, int):
                        dve.wait_ge(gathered, 16 * GATHERS * (2 * r + u + 2))
                    else:
                        dve.wait_ge(gathered, r * (32 * GATHERS) + 16 * GATHERS * (u + 2))
                    for s in range(GATHERS):
                        last = stt(x2[:, t], gb[:, s], wf[:, t, s:s + 1], x2[:, t], ALU.mult, ALU.add)
                        if s < GATHERS - 1:
                            dve.drain()
                    last.then_inc(S["x2_ready"], 1)
                    dve.drain()
                    stats(x2[:, t], st2, mv2, c2, "stats2")
                if has(r, u, 0):
                    upto(dve, "hT_hi", r, u, 0)
                    V.tensor_tensor(hT[:, 1].rearrange("p c h -> p (c h)"), tr[:, 1],
                                    hT[:, 0].rearrange("p c h -> p (c h)"), ALU.subtract).then_inc(S["hT_lo"], 1)
                if has(r, u, 2):
                    upto(dve, "pT_hi", r, u, 2)
                    V.tensor_tensor(pT[:, 1].rearrange("p c h -> p (c h)"), tr[:, 0],
                                    pT[:, 0].rearrange("p c h -> p (c h)"), ALU.subtract).then_inc(S["pT_lo"], 1)
                    upto(dve, "o_copied", r, u, 2)
                    V.tensor_tensor(cb[:, 0:M], fe[:, 0, 0:M], osb[:, :], ALU.add)
                    V.tensor_tensor(cb[:, HALF:Q:-1], fe[:, 0, 0:Q], osb[:, 0:Q], ALU.subtract)
                    dve.drain().then_inc(S["corr_done"], 1)
                    V.max(m8[:, :], cb[:, 1:HALF + 1])
                    dve.drain()
                    V.max_index(i8[:, :], m8[:, :], cb[:, 1:HALF + 1])
                    dve.drain()
                    ts(lag[:, 0:3], i8[:, 0:3], 1.0, None, ALU.add)
                    ts(mir[:, :], i8[:, 0:3], -1.0, float(L - 1), ALU.mult, ALU.add)
                    ts(own[:, :], i8[:, 0:2], float(HALF - 1), None, ALU.is_equal)
                    dve.drain()
                    ts(notown[:, :], own[:, :], -1.0, 1.0, ALU.mult, ALU.add)
                    dve.drain()
                    V.tensor_tensor(keep[:, 0:2], notown[:, :], mir[:, 0:2], ALU.mult)
                    V.tensor_tensor(keep[:, 2:4], notown[:, :], m8[:, 0:2], ALU.mult)
                    V.tensor_copy(val[:, 0:3], m8[:, 0:3])
                    V.tensor_copy(val[:, 5:6], cb[:, 0:1])
                    ts(nv0[:, :], cb[:, 0:1], -1.0)
                    dve.drain()
                    stt(lag[:, 3:5], own[:, :], mir[:, 2:3], keep[:, 0:2], ALU.mult, ALU.add)
                    stt(val[:, 3:5], own[:, :], m8[:, 2:3], keep[:, 2:4], ALU.mult, ALU.add)
                    dve.drain().then_inc(S["vals_ready"], 1)
                if has(r, u, 1):
                    t = (u + 1) % 2
                    upto(dve, "xT_hi", r, u, 1)
                    V.tensor_tensor(xT[:, t, 1].rearrange("p c h -> p (c h)"), tr[:, :, :].rearrange("p a b -> p (a b)"),
                                    xT[:, t, 0].rearrange("p c h -> p (c h)"), ALU.subtract).then_inc(S["xT_lo"], 1)
            steps(dve, step)

        @block.tensor
        def _(pe):
            mm = nc.tensor.matmul
            PASSES = ((0, 0), (0, 1), (1, 0))

            def down_and_scores(x):
                for c in range(IC):
                    for a, b in PASSES:
                        first, last = c == 0 and (a, b) == (0, 0), c == IC - 1 and a == 1
                        mm(hps[:, :], x[:, a, c], d16[:, b, c], start=first, stop=last)
                        m = mm(small[:, 0:E], x[:, a, c], kq16[:, b, c], start=first, stop=last)
                return m

            def base(x, chunks):
                for c in chunks:
                    for a, b in PASSES:
                        for o in range(2):
                            m = mm(acc[:, o], x[:, a, c], w16[:, b, c, o * 512:(o + 1) * 512],
                                   start=c == 0 and (a, b) == (0, 0), stop=False, skip_group_check=True)
                return m

            def lora_up():
                for c in range(RC):
                    for a, b in PASSES:
                        for o in range(2):
                            m = mm(acc[:, o], hT[:, a, c], u16[:, b, c, o * 512:(o + 1) * 512],
                                   start=False, stop=c == RC - 1 and a == 1, skip_group_check=True)
                return m

            def forward():
                for part in range(4):
                    for c in range(2):
                        for a, b in PASSES:
                            m = mm(fe[:, part // 2, (part % 2) * Q:(part % 2 + 1) * Q], foT[:, a, 2 * part + c],
                                   fwd[:, b, 2 * part + c], start=c == 0 and (a, b) == (0, 0), stop=c == 1 and a == 1)
                return m

            def backward():
                for part in range(2):
                    for c in range(2):
                        for a, b in PASSES:
                            m = mm(fe[:, part, 0:M], pT[:, a, 2 * part + c], inv[:, b, 2 * part + c],
                                   start=c == 0 and (a, b) == (0, 0), stop=c == 1 and a == 1)
                return m

            def transposes(dst, src, count):
                for c in range(count):
                    m = nc.tensor.transpose(dst[:, c * P:(c + 1) * P], src[:, c * P:(c + 1) * P], ident[:, :])
                return m

            tr_flat = tr[:, :, :].rearrange("p a b -> p (a b)")
            pe.wait_ge(const_ready, 4)

            def step(r, u):
                x = xT[:, u]
                if has(r, u, 0):
                    upto(pe, "xT_lo", r, u, 0)
                    upto(pe, "hs_ready", r, u, -1)
                    down_and_scores(x).then_inc(S["ds_done"], 1)
                if has(r, u, 2):
                    a = (u + 2) % 2
                    upto(pe, "fold_odd", r, u, 2, 2)
                    upto(pe, "even_folded", r, u, 2)
                    upto(pe, "xT_lo", r, u, 0)
                    transposes(tr_flat, fo[:, a].rearrange("p a b -> p (a b)"), 8).then_inc(S["t1_done"], 1)
                if has(r, u, 0):
                    upto(pe, "out_ready", r, u, -1)
                    base(x, range(0, 3))
                    upto(pe, "s_copied", r, u, 0)
                    mm(small[:, E:2 * E], mean_of[:, :], sc[:, :], start=True, stop=True).then_inc(S["mean_done"], 1)
                if has(r, u, 2):
                    upto(pe, "foT_lo", r, u, 2)
                    upto(pe, "corr_done", r, u, 1)
                    forward().then_inc(S["f_done"], 1)
                if has(r, u, 0):
                    base(x, range(3, 5))
                    upto(pe, "hs_ready", r, u, 0)
                    if has(r, u, 2):
                        upto(pe, "foT_lo", r, u, 2)
                    transposes(tr[:, 1], hs[:, :], RC).then_inc(S["h_tr"], 1)
                if has(r, u, 2):
                    upto(pe, "p_ready", r, u, 2)
                    transposes(tr[:, 0], pw[:, :], 4).then_inc(S["t2_done"], 1)
                if has(r, u, 0):
                    base(x, range(5, 7))
                if has(r, u, 2):
                    upto(pe, "pT_lo", r, u, 2)
                    upto(pe, "sq_done", r, u, 2)
                    backward().then_inc(S["i_done"], 1)
                if has(r, u, 0):
                    base(x, range(7, 8)).then_inc(S["base_done"], 1)
                if has(r, u, 1):
                    upto(pe, "x2n_ready", r, u, 1)
                    if has(r, u, 2):
                        upto(pe, "pT_lo", r, u, 2)
                    if has(r, u, 0):
                        upto(pe, "hT_lo", r, u, 0)
                    transposes(tr_flat, x2n[:, :], 8).then_inc(S["t3_done"], 1)
                if has(r, u, 0):
                    upto(pe, "hT_lo", r, u, 0)
                    lora_up().then_inc(S["acc_done"], 1)
            steps(pe, step)


def kernel(**inputs):
    import concourse.bacc as bacc
    from concourse.bass_utils import run_bass_kernel_spmd

    x = inputs["x"]
    part = np.transpose(x, (3, 2, 1, 0))
    fwd_c, inv_c = dft_constants()
    down = np.transpose(inputs["L0_ffn_lora_down"], (1, 0, 2)).reshape(L, ER)
    arrays = {
        "w_re": np.concatenate([part[0], part[0]]), "w_im": np.concatenate([part[1], part[1]]),
        "log_dt": inputs["L0_tok_log_dt"].T,
        "lam": np.concatenate([inputs["L0_tok_Lambda"]] * 2),
        "w_org": inputs["L0_ffn_W_org"].T, "down": down,
        "up": inputs["L0_ffn_lora_up"].reshape(ER, L), "keys": inputs["L0_ffn_lora_keys"].T,
        "wq": inputs["L0_ffn_Wq"],
        "fwd": fwd_c, "inv": inv_c, "eye": np.eye(P, dtype=np.float32),
    }
    arrays = {k: np.ascontiguousarray(a) for k, a in arrays.items()}
    nc = bacc.Bacc("TRN2", target_bir_lowering=False, num_devices=1)
    args = [nc.dram_tensor(f"in_{k}", a.shape, mybir.dt.from_np(a.dtype), kind="ExternalInput").ap()
            for k, a in arrays.items()]
    out = nc.dram_tensor("out", (NT, H, L), F32, kind="ExternalOutput").ap()
    vit_tower(nc, *args, out)
    r = run_bass_kernel_spmd(nc, [{f"in_{k}": a for k, a in arrays.items()}], core_ids=[0])
    return r.results[0]["out"]
```

```python
from contextlib import ExitStack

import numpy as np

import concourse.bass as bass
from concourse import mybir

F32 = mybir.dt.float32
F16 = mybir.dt.float16
U32 = mybir.dt.uint32
I32 = mybir.dt.int32
ALU = mybir.AluOpType
ACT = mybir.ActivationFunctionType
AX = mybir.AxisListType.X
RMAX = bass.bass_isa.ReduceOp.max

P = 128
NT = 64
H = 128
N = 64
L = 1024
HALF = L // 2
PARTS = 4
PART = L // PARTS
E, R, KEY = 8, 64, 128
ER = E * R
IC = L // P
RC = ER // P
Q = 256
M = 257
MS = 258
ROW = 2 * L
LN_EPS = 1e-5
REC_EPS = 1e-7
ROUND = 12582912.0
TURN = 6.283185
HB = 8
NB = H // HB
GATHERS = 5
GROW, SIGN, LOWER, UPPER, NLOWER, PHASE, SHIFT = range(7)


def split16(a):
    hi = a.astype(np.float16)
    return hi, (a - hi.astype(np.float64)).astype(np.float16)


def dft_constants():
    w = 2 * np.pi / L
    l0, l1 = np.arange(Q)[:, None], np.arange(1, Q + 1)[:, None]
    even, odd = 2 * np.arange(Q)[None] + 2, 2 * np.arange(Q)[None] + 1
    re_even = np.cos(w * (l0 * even % L)) - np.cos(w * (Q * even % L))
    re_odd = np.cos(w * (l0 * odd % L))
    im_even = np.sin(w * (l1 * even % L))
    im_odd = np.sin(w * (l1 * odd % L))
    im_odd[-1] *= 0.5
    fwd = np.concatenate([re_even, re_odd, im_even, im_odd]).reshape(8, P, Q).transpose(1, 0, 2)
    m = np.arange(M)[None]
    weight = np.where(even.T == HALF, 1.0, 2.0)
    inv = np.concatenate([weight * np.cos(w * (even.T * m % L)), 2 * np.cos(w * (odd.T * m % L))])
    inv = np.pad(inv, ((0, 0), (0, MS - M))).reshape(4, P, MS).transpose(1, 0, 2)
    return np.stack(split16(fwd), 1), np.stack(split16(inv), 1)


def vit_tower(nc, wre, wim, log_dt, lam, w_org, down, up, keys, wq, fwd_c, inv_c, eye, out):
    with ExitStack() as ctx:
        def sb(name, shape, dt=F32):
            return ctx.enter_context(nc.sbuf_tensor(name, shape, dt))

        def sem(name):
            return ctx.enter_context(nc.semaphore(name))

        twice = nc.dram_tensor("k_twice", (NT * H * ROW, 1), F32, kind="Internal").ap()
        by_row = twice.rearrange("(r n) o -> r (n o)", n=ROW)
        by_half = twice.rearrange("(c h w a b) o -> w a c h (b o)", c=NT, h=H, w=2, a=2)
        out_rows = out.rearrange("c h l -> (c h) l")

        ident = sb("ident", [P, P])
        w16 = sb("w16", [P, 2, IC, L], F16)
        d16 = sb("d16", [P, 2, IC, ER], F16)
        kq16 = sb("kq16", [P, 2, IC, E], F16)
        fwd = sb("fwd", [P, 2, 8, Q], F16)
        inv = sb("inv", [P, 2, 4, MS], F16)
        scale = sb("scale", [P, 8])
        zr = sb("zr", [P, H])
        turns = sb("turns", [P, H])
        s1 = sb("s1", [P, PARTS, H])
        s2 = sb("s2", [P, PARTS, H])
        pos = sb("pos", [P, PART])
        side = sb("side", [P, SHIFT + PARTS])

        tables(nc, locals())
        generate(nc, locals())
        tower(nc, locals())


def tables(nc, v):
    ident, w16, d16, kq16, fwd, inv, scale = (v[k] for k in ("ident", "w16", "d16", "kq16", "fwd", "inv", "scale"))
    zr, turns, s1, s2, pos, side = (v[k] for k in ("zr", "turns", "s1", "s2", "pos", "side"))
    w_org, down, up, keys, wq, log_dt, lam = (v[k] for k in ("w_org", "down", "up", "keys", "wq", "log_dt", "lam"))
    with ExitStack() as ctx:
        def sb(name, shape, dt=F32):
            return ctx.enter_context(nc.sbuf_tensor(name, shape, dt))

        def sem(name):
            return ctx.enter_context(nc.semaphore(name))

        wf = sb("wf", [P, IC, L])
        df = sb("df", [P, IC, ER])
        uf = sb("uf", [P, RC, L])
        wqf = sb("wqf", [P, L])
        keysf = sb("keysf", [P, E])
        kqf = sb("kqf", [P, IC, E])
        peak = sb("peak", [P, 4])
        top = sb("top", [P, 4])
        power = sb("power", [P, 4])
        rawscale = sb("rawscale", [P, 5])
        lamf = sb("lamf", [P, 2])
        dt = sb("dt", [P, 2, H])
        z = sb("z", [P, 2, H])
        zneg = sb("zneg", [P, 2, H])
        tin = sb("tin", [P, 2, H])
        th = sb("th", [P, 2, H])
        ein = sb("ein", [P, PARTS, H])
        ex = sb("ex", [P, PARTS, H])
        ang = sb("ang", [P, 4 + 2 * PARTS, H])
        whole = sb("whole", [P, 4 + 2 * PARTS, H])
        sn = sb("sn", [P, 4 + 2 * PARTS, H])
        rot = sb("rot", [P, 2, PARTS, H])
        wk = [sb(f"wk{i}", [P, 2, H]) for i in range(6)]
        re, im = sb("re", [P, 2, H]), sb("im", [P, 2, H])
        q = [sb(f"q{i}", [P, H]) for i in range(10)]
        ps_kq = ctx.enter_context(nc.psum_tensor("ps_kq", [P, IC * E], F32))

        loaded = sem("loaded")
        wq_loaded = sem("wq_loaded")
        kq_done = sem("kq_done")
        kq_copied = sem("kq_copied")
        peaks_ready = sem("peaks_ready")
        top_ready = sem("top_ready")
        scale_ready = sem("scale_ready")
        hi_ready = sem("hi_ready")
        small_loaded = sem("small_loaded")
        dt_ready = sem("dt_ready")
        args_ready = sem("args_ready")
        funcs_ready = sem("funcs_ready")
        pos_ready = sem("pos_ready")
        block = ctx.enter_context(nc.Block())

        @block.sync
        def _(sp):
            sp.dma_start(dt[:, 0, :], log_dt[0:1, :].partition_broadcast(P)).then_inc(small_loaded, 16)
            sp.dma_start(dt[:, 1, :], log_dt[1:2, :].partition_broadcast(P)).then_inc(small_loaded, 16)
            sp.dma_start(lamf[:, :], lam).then_inc(small_loaded, 16)
            sp.dma_start(wqf[:, :], wq).then_inc(wq_loaded, 16)
            sp.dma_start(keysf[:, :], keys).then_inc(wq_loaded, 16)
            sp.dma_start(wf[:, :, :], w_org.rearrange("(c p) o -> p c o", p=P)).then_inc(loaded, 16)
            sp.dma_start(df[:, :, :], down.rearrange("(c p) o -> p c o", p=P)).then_inc(loaded, 16)
            sp.dma_start(uf[:, :, :], up.rearrange("(c p) o -> p c o", p=P)).then_inc(loaded, 16)
            sp.dma_start(ident[:, :], v["eye"]).then_inc(loaded, 16)
            sp.dma_start(fwd[:, :, :, :], v["fwd_c"]).then_inc(loaded, 16)
            sp.dma_start(inv[:, :, :, :], v["inv_c"]).then_inc(loaded, 16)
            sp.wait_ge(loaded, 96)

        @block.tensor
        def _(pe):
            pe.wait_ge(wq_loaded, 32)
            for c in range(IC):
                last = nc.tensor.matmul(ps_kq[:, c * E:(c + 1) * E], wqf[:, c * P:(c + 1) * P], keysf[:, :],
                                        start=True, stop=True)
            last.then_inc(kq_done, 1)

        @block.gpsimd
        def _(pool):
            nc.gpsimd.iota(pos[:, :], [[1, PART]], base=0, channel_multiplier=0,
                           allow_small_or_imprecise_dtypes=True).then_inc(pos_ready, 1)
            pool.wait_ge(peaks_ready, 1)
            nc.gpsimd.partition_all_reduce(top[:, :], peak[:, :], P, RMAX).then_inc(top_ready, 1)

        @block.scalar
        def _(act):
            act.wait_ge(small_loaded, 48)
            nc.scalar.activation(dt[:, :, :], dt[:, :, :], ACT.Exp).then_inc(dt_ready, 1)
            act.wait_ge(args_ready, 1)
            nc.scalar.activation(th[:, :, :], tin[:, :, :], ACT.Tanh).then_inc(funcs_ready, 1)
            nc.scalar.activation(ex[:, :, :], ein[:, :, :], ACT.Exp).then_inc(funcs_ready, 1)
            nc.scalar.activation(sn[:, :, :], ang[:, :, :], ACT.Sin, scale=TURN).then_inc(funcs_ready, 1)
            act.wait_ge(kq_done, 1)
            nc.scalar.activation(kqf[:, :, :], ps_kq[:, :].rearrange("p (c e) -> p c e", e=E), ACT.Copy)\
                .then_inc(kq_copied, 1)
            act.wait_ge(scale_ready, 1)
            nc.scalar.activation(w16[:, 0], wf[:, :, :], ACT.Copy, scale=scale[:, 0:1]).then_inc(hi_ready, 1)
            nc.scalar.activation(d16[:, 0], df[:, :, :], ACT.Copy, scale=scale[:, 1:2]).then_inc(hi_ready, 1)
            nc.scalar.activation(kq16[:, 0], kqf[:, :, :], ACT.Copy, scale=scale[:, 3:4]).then_inc(hi_ready, 1)

        @block.vector
        def _(dve):
            V = nc.vector

            def ts(out, in0, a, b=None, op0=ALU.mult, op1=ALU.bypass):
                V.tensor_scalar(out, in0, a, b, op0, op1)

            V.memset(side[:, :], 0.0)
            dve.drain()
            V.memset(side[0:N, LOWER:LOWER + 1], 1.0)
            V.memset(side[N:P, UPPER:UPPER + 1], 1.0)
            V.memset(side[0:N, NLOWER:NLOWER + 1], -1.0)
            V.memset(side[0:N, PHASE:PHASE + 1], 0.25)
            dve.wait_ge(small_loaded, 48)
            ts(side[:, GROW:GROW + 1], lamf[:, 0:1], 0.0, None, ALU.is_gt)
            dve.drain()
            ts(side[:, SIGN:SIGN + 1], side[:, GROW:GROW + 1], -2.0, 1.0, ALU.mult, ALU.add)
            for a in range(PARTS):
                ts(side[:, SHIFT + a:SHIFT + a + 1], side[:, GROW:GROW + 1], -float(L - PART), float(PART * a),
                   ALU.mult, ALU.add)
            dve.wait_ge(pos_ready, 1)
            ts(power[:, 0:1], side[:, GROW:GROW + 1], -float(PART - 1))
            dve.drain()
            ts(pos[:, :], pos[:, :], power[:, 0:1], None, ALU.add)

            dve.wait_ge(dt_ready, 1)
            for k in range(2):
                ts(z[:, k], dt[:, k], lamf[:, k:k + 1])
            dve.drain()
            ts(zneg[:, :, :], z[:, :, :], side[:, SIGN:SIGN + 1])
            V.tensor_copy(zr[:, :], z[:, 0])
            ts(turns[:, :], z[:, 1], 1.0 / (2 * np.pi))
            dve.drain()
            for k, times in enumerate((1, L)):
                ts(tin[:, k], zneg[:, 0], 0.5 * times)
                ts(ang[:, 2 * k], zneg[:, 1], times / (4 * np.pi))
                ts(ang[:, 2 * k + 1], zneg[:, 1], times / (4 * np.pi), 0.25, ALU.mult, ALU.add)
            for a in range(PARTS):
                f = side[:, SHIFT + a:SHIFT + a + 1]
                ts(ein[:, a], z[:, 0], f)
                ts(ang[:, 4 + 2 * a], turns[:, :], f)
                ts(ang[:, 5 + 2 * a], turns[:, :], f, 0.25, ALU.mult, ALU.add)
            dve.drain()
            ts(whole[:, :, :], ang[:, :, :], ROUND, -ROUND, ALU.add, ALU.add)
            dve.drain()
            V.tensor_tensor(ang[:, :, :], ang[:, :, :], whole[:, :, :], ALU.subtract)
            dve.drain().then_inc(args_ready, 1)

            dve.wait_ge(funcs_ready, 3)
            sin_half, cos_half = sn[:, 0:4:2], sn[:, 1:4:2]
            ts(wk[0][:, :, :], th[:, :, :], -1.0, 1.0, ALU.mult, ALU.add)
            V.scalar_tensor_tensor(wk[2][:, :, :], sin_half, -2.0, sin_half, ALU.mult, ALU.mult)
            V.scalar_tensor_tensor(wk[3][:, :, :], sin_half, 2.0, cos_half, ALU.mult, ALU.mult)
            dve.drain()
            V.reciprocal(wk[1][:, :, :], wk[0][:, :, :])
            dve.drain()
            V.scalar_tensor_tensor(wk[4][:, :, :], th[:, :, :], 2.0, wk[1][:, :, :], ALU.mult, ALU.mult)
            dve.drain()
            V.scalar_tensor_tensor(wk[5][:, :, :], wk[2][:, :, :], 1.0, wk[4][:, :, :], ALU.add, ALU.mult)
            V.scalar_tensor_tensor(im[:, :, :], wk[4][:, :, :], 1.0, wk[3][:, :, :], ALU.add, ALU.mult)
            dve.drain()
            V.tensor_tensor(re[:, :, :], wk[5][:, :, :], wk[2][:, :, :], ALU.add)
            dve.drain()
            lr, li = lamf[:, 0:1], lamf[:, 1:2]
            ts(q[0][:, :], im[:, 1], li)
            ts(q[1][:, :], im[:, 1], lr)
            dve.drain()
            V.scalar_tensor_tensor(q[2][:, :], re[:, 1], lr, q[0][:, :], ALU.mult, ALU.subtract)
            V.scalar_tensor_tensor(q[3][:, :], re[:, 1], li, q[1][:, :], ALU.mult, ALU.add)
            dve.drain()
            V.tensor_tensor(q[4][:, :], q[2][:, :], q[2][:, :], ALU.mult)
            V.tensor_tensor(q[5][:, :], q[3][:, :], q[3][:, :], ALU.mult)
            V.tensor_tensor(q[6][:, :], re[:, 0], q[2][:, :], ALU.mult)
            V.tensor_tensor(q[7][:, :], im[:, 0], q[3][:, :], ALU.mult)
            V.tensor_tensor(q[8][:, :], im[:, 0], q[2][:, :], ALU.mult)
            V.tensor_tensor(q[9][:, :], re[:, 0], q[3][:, :], ALU.mult)
            dve.drain()
            V.scalar_tensor_tensor(q[0][:, :], q[4][:, :], REC_EPS, q[5][:, :], ALU.add, ALU.add)
            dve.drain()
            V.reciprocal(q[1][:, :], q[0][:, :])
            V.tensor_tensor(q[2][:, :], q[6][:, :], q[7][:, :], ALU.add)
            V.tensor_tensor(q[3][:, :], q[8][:, :], q[9][:, :], ALU.subtract)
            dve.drain()
            V.tensor_tensor(q[4][:, :], q[2][:, :], q[1][:, :], ALU.mult)
            V.tensor_tensor(q[5][:, :], q[3][:, :], q[1][:, :], ALU.mult)
            V.tensor_tensor(rot[:, 0], ex[:, :, :], sn[:, 5:4 + 2 * PARTS:2], ALU.mult)
            V.tensor_tensor(rot[:, 1], ex[:, :, :], sn[:, 4:4 + 2 * PARTS:2], ALU.mult)
            dve.drain()
            for a in range(PARTS):
                V.tensor_tensor(q[6][:, :], q[4][:, :], rot[:, 0, a], ALU.mult)
                V.tensor_tensor(q[7][:, :], q[5][:, :], rot[:, 1, a], ALU.mult)
                V.tensor_tensor(q[8][:, :], q[4][:, :], rot[:, 1, a], ALU.mult)
                V.tensor_tensor(q[9][:, :], q[5][:, :], rot[:, 0, a], ALU.mult)
                dve.drain()
                V.tensor_tensor(q[0][:, :], q[6][:, :], q[7][:, :], ALU.subtract)
                V.tensor_tensor(q[1][:, :], q[8][:, :], q[9][:, :], ALU.add)
                dve.drain()
                ts(q[2][:, :], q[1][:, :], side[:, UPPER:UPPER + 1])
                ts(q[3][:, :], q[0][:, :], side[:, UPPER:UPPER + 1])
                dve.drain()
                V.scalar_tensor_tensor(s1[:, a], q[0][:, :], side[:, LOWER:LOWER + 1], q[2][:, :], ALU.mult, ALU.subtract)
                V.scalar_tensor_tensor(s2[:, a], q[1][:, :], side[:, NLOWER:NLOWER + 1], q[3][:, :], ALU.mult, ALU.subtract)
                dve.drain()

            dve.wait_ge(loaded, 96)
            dve.wait_ge(kq_copied, 1)
            for k, t in enumerate((wf, df, uf, kqf)):
                flat = t[:, :, :].rearrange("p a b -> p (a b)")
                V.tensor_reduce(peak[:, k:k + 1], flat, axis=AX, op=ALU.max, apply_absolute_value=True)
            dve.drain().then_inc(peaks_ready, 1)
            dve.wait_ge(top_ready, 1)
            V.tensor_scalar(power[:, :].bitcast(I32), top[:, :].bitcast(I32), 0x7F800000, None, ALU.bitwise_and)
            dve.drain()
            ts(power[:, :], power[:, :], 2.0 ** -60, None, ALU.max)
            dve.drain()
            V.reciprocal(rawscale[:, 0:4], power[:, :])
            dve.drain()
            V.tensor_copy(scale[:, 1:2], rawscale[:, 1:2])
            V.tensor_copy(scale[:, 3:4], rawscale[:, 3:4])
            V.tensor_tensor(rawscale[:, 4:5], rawscale[:, 1:2], rawscale[:, 2:3], ALU.mult)
            ts(scale[:, 5:6], power[:, 3:4], 1.0 / np.sqrt(KEY))
            dve.drain()
            V.tensor_tensor(scale[:, 0:1], rawscale[:, 0:1], rawscale[:, 4:5], ALU.min)
            dve.drain()
            V.tensor_tensor(scale[:, 2:3], scale[:, 0:1], power[:, 1:2], ALU.mult)
            V.reciprocal(scale[:, 4:5], scale[:, 0:1])
            dve.drain().then_inc(scale_ready, 1)
            for k, (t, t16) in enumerate(((wf, w16), (df, d16), (kqf, kq16))):
                dve.wait_ge(hi_ready, k + 1)
                col = (0, 1, 3)[k]
                V.scalar_tensor_tensor(t16[:, 1], t[:, :, :], scale[:, col:col + 1], t16[:, 0], ALU.mult, ALU.subtract)


def generate(nc, v):
    zr, turns, s1, s2, pos, side = (v[k] for k in ("zr", "turns", "s1", "s2", "pos", "side"))
    wre, wim, by_half = v["wre"], v["wim"], v["by_half"]
    HG = HB // 2
    with ExitStack() as ctx:
        def sb(name, shape, dt=F32):
            return ctx.enter_context(nc.sbuf_tensor(name, shape, dt))

        def sem(name):
            return ctx.enter_context(nc.semaphore(name))

        wa = sb("wa", [P, 2, HB, N])
        wb = sb("wb", [P, 2, HB, N])
        pr = sb("pr", [P, HB, 2, 2, N])
        wp = sb("wp", [P, 2, HB, 2, 2, N])
        zrb = sb("zrb", [P, 2, HB])
        tub = sb("tub", [P, 2, HB])
        ang = sb("angle", [P, 2, HB, PART])
        whole = sb("whole_turns", [P, HB, PART])
        amp = sb("amp", [P, 2, HB, PART])
        wav = sb("wav", [P, 2, HB, PART])
        kst = sb("kst", [P, 2, HG, HALF])
        ps = ctx.enter_context(nc.psum_tensor("ps_k", [P, HB, HALF], F32))

        w_loaded = [sem(f"w_loaded{u}") for u in range(2)]
        par_ready = sem("par_ready")
        exp_done = sem("exp_done")
        whole_ready = sem("whole_ready")
        part_ready = sem("part_ready")
        sin_done = sem("sin_done")
        wave_ready = sem("wave_ready")
        pr_ready = sem("pr_ready")
        wp_ready = sem("wp_ready")
        k_done = sem("k_done")
        copied = sem("copied")
        stored = [sem(f"stored{g}") for g in range(2)]
        block = ctx.enter_context(nc.Block())

        def blocks(eng, body):
            body(0, 0)
            body(0, 1)
            with eng.Fori(1, NB // 2) as r:
                body(r, 0)
                body(r, 1)

        def has(r, u, off):
            return not isinstance(r, int) or 2 * r + u + off >= 0

        def upto(eng, sm, r, u, off, per=1):
            if isinstance(r, int):
                if 2 * r + u + off >= 0:
                    eng.wait_ge(sm, per * (2 * r + u + off + 1))
            else:
                eng.wait_ge(sm, r * (2 * per) + per * (u + off + 1))

        def rows_of(r, u):
            b = (2 * r + u) * HB if isinstance(r, int) else r * (2 * HB) + u * HB
            return bass.ds(b, HB)

        def factor(t, r, u, a):
            return t[:, a, rows_of(r, u)].unsqueeze(2).broadcast_to([P, HB, N])

        @block.sync
        def _(sp):
            def load_next(r, u):
                static = isinstance(r, int)
                h2 = (2 * r + u + 2) * HB if static else sp.snap(r * (2 * HB) + (u + 2) * HB)
                need = 2 * r + u + 1 if static else sp.snap(r * 2 + (u + 1))
                for w_s, src in ((wa, wre), (wb, wim)):
                    sp.wait_ge(wp_ready, need)
                    sp.dma_start(w_s[:, u], src[:, bass.ds(h2, HB), :]).then_inc(w_loaded[u], 16)

            def store(r, u, off):
                def number(per, add):
                    add += (u + off) * per
                    return 2 * r * per + add if isinstance(r, int) else sp.snap(r * (2 * per) + add)

                rows = [number(HB, g * HG) for g in range(2)]
                need = [number(HB, (g + 1) * HG) for g in range(2)]
                for g in range(2):
                    for w in range(2):
                        for a in range(2):
                            sp.wait_ge(copied, need[g])
                            sp.dma_start(by_half[w, a, :, bass.ds(rows[g], HG), :],
                                         kst[a * N:(a + 1) * N, g]).then_inc(stored[g], 16)

            for u in range(2):
                for w_s, src in ((wa, wre), (wb, wim)):
                    sp.dma_start(w_s[:, u], src[:, u * HB:(u + 1) * HB, :]).then_inc(w_loaded[u], 16)
            for u in range(2):
                load_next(0, u)
            with sp.Fori(1, NB // 2 - 1) as r:
                for u in range(2):
                    load_next(r, u)
                    store(r, u, -2)
            for b in range(NB - 4, NB):
                store(b // 2, b % 2, 0)
            for g in range(2):
                sp.wait_ge(stored[g], 64 * NB)

        @block.gpsimd
        def _(pool):
            def body(r, u):
                upto(pool, wp_ready, r, u, -1)
                pool.wait_ge(w_loaded[u], 32 * (r + 1) if isinstance(r, int) else r * 32 + 32)
                for a in range(PARTS):
                    nc.gpsimd.tensor_tensor(pr[:, :, a % 2, a // 2], wb[:, u], factor(s2, r, u, a), ALU.mult)\
                        .then_inc(pr_ready, 1)
                upto(pool, whole_ready, r, u, 0)
                nc.gpsimd.tensor_tensor(ang[:, u], ang[:, u], whole[:, :, :], ALU.subtract).then_inc(part_ready, 1)
            blocks(pool, body)

        @block.scalar
        def _(act):
            def copies(r, u, off):
                for j in range(HB):
                    upto(act, k_done, r, u, off)
                    if j % HG == 0:
                        upto(act, stored[j // HG], r, u, off - 1, 64)
                    nc.scalar.activation(kst[:, j // HG, j % HG], ps[:, j], ACT.Copy).then_inc(copied, 1)

            def body(r, u):
                upto(act, par_ready, r, u, 0)
                upto(act, wave_ready, r, u, -2)
                for j in range(HB):
                    last = nc.scalar.activation(amp[:, u, j], pos[:, :], ACT.Exp, scale=zrb[:, u, j:j + 1])
                last.then_inc(exp_done, 1)
                if has(r, u, -2):
                    copies(r, u, -2)
                upto(act, part_ready, r, u, 0)
                nc.scalar.activation(ang[:, u], ang[:, u], ACT.Sin, scale=TURN).then_inc(sin_done, 1)
            blocks(act, body)
            copies(NB // 2, 0, -2)
            copies(NB // 2, 0, -1)

        @block.vector
        def _(dve):
            V = nc.vector

            def angles(r, u):
                upto(dve, exp_done, r, u, -2)
                V.tensor_copy(zrb[:, u], zr[:, rows_of(r, u)])
                V.tensor_copy(tub[:, u], turns[:, rows_of(r, u)])
                dve.drain().then_inc(par_ready, 1)
                for j in range(HB):
                    V.tensor_scalar(ang[:, u, j], pos[:, :], tub[:, u, j:j + 1], side[:, PHASE:PHASE + 1],
                                    ALU.mult, ALU.add)
                dve.drain()
                upto(dve, part_ready, r, u, -1)
                V.tensor_scalar(whole[:, :, :], ang[:, u], ROUND, -ROUND, ALU.add, ALU.add).then_inc(whole_ready, 1)

            def wave(r, u, off):
                w = (u + off) % 2
                upto(dve, k_done, r, u, off - 2)
                upto(dve, exp_done, r, u, off)
                upto(dve, sin_done, r, u, off)
                V.tensor_tensor(wav[:, w], amp[:, w], ang[:, w], ALU.mult).then_inc(wave_ready, 1)

            def stationary(r, u):
                dve.wait_ge(w_loaded[u], 32 * (r + 1) if isinstance(r, int) else r * 32 + 32)
                upto(dve, k_done, r, u, -2)
                for a in range(PARTS):
                    V.tensor_tensor(wp[:, u, :, a % 2, a // 2], wa[:, u], factor(s1, r, u, a), ALU.mult)
                dve.drain()
                upto(dve, pr_ready, r, u, 0, PARTS)
                V.tensor_tensor(wp[:, u], wp[:, u], pr[:, :], ALU.add).then_inc(wp_ready, 1)

            def body(r, u):
                angles(r, u)
                if has(r, u, -1):
                    wave(r, u, -1)
                stationary(r, u)
            blocks(dve, body)
            wave(NB // 2, 0, -1)

        @block.tensor
        def _(pe):
            def body(r, u):
                upto(pe, wp_ready, r, u, 0)
                upto(pe, wave_ready, r, u, 0)
                upto(pe, copied, r, u, -1, HB)
                for j in range(HB):
                    for q in range(2):
                        last = nc.tensor.matmul(ps[:, j, q * PART:(q + 1) * PART],
                                                wp[:, u, j, q].rearrange("p a c -> p (a c)"), wav[:, u, j],
                                                start=True, stop=True)
                last.then_inc(k_done, 1)
            blocks(pe, body)


def tower(nc, v):
    ident, w16, d16, kq16, fwd, inv, scale = (v[k] for k in ("ident", "w16", "d16", "kq16", "fwd", "inv", "scale"))
    twice, by_row, out_rows, up = v["twice"], v["by_row"], v["out_rows"], v["up"]
    with ExitStack() as ctx:
        def sb(name, shape, dt=F32):
            return ctx.enter_context(nc.sbuf_tensor(name, shape, dt))

        def sem(name):
            return ctx.enter_context(nc.semaphore(name))

        u16 = sb("u16", [P, 2, RC, L], F16)
        kt = sb("kt", [P, 2, L])
        xn = sb("xn", [P, L])
        evn = sb("evn", [P, HALF + 1])
        odd = sb("odd", [P, HALF])
        fo = sb("fo", [P, 2, 4, Q])
        foT = sb("foT", [P, 2, 8, P], F16)
        sq = sb("sq", [P, 2, HALF])
        pw = sb("pw", [P, HALF])
        pT = sb("pT", [P, 2, 4, P], F16)
        osb = sb("osb", [P, M])
        cb = sb("cb", [P, HALF + 1])
        gb = sb("gb", [P, GATHERS, L])
        x2 = sb("x2", [P, 2, L])
        x2n = sb("x2n", [P, L])
        xT = sb("xT", [P, 2, 2, IC, P], F16)
        hs = sb("hs", [P, ER])
        hT = sb("hT", [P, 2, RC, P], F16)
        mean_of = sb("mean_of", [P, P])
        sc = sb("sc", [P, E])
        ex8 = sb("ex8", [P, E])
        soft = sb("soft", [P, 4])
        st = sb("st", [P, 12])
        mv = sb("mv", [P, 2])
        st2 = sb("st2", [P, 12])
        mv2 = sb("mv2", [P, 2])
        c1 = sb("c1", [P, 2, 2])
        n1 = sb("n1", [P, 2, 2])
        nk = sb("nk", [P, 2])
        c2 = sb("c2", [P, 2])
        n2 = sb("n2", [P, 2])
        mhalf = sb("mhalf", [P, 1])
        m8 = sb("m8", [P, 8])
        i8 = sb("i8", [P, 8], U32)
        lag = sb("lag", [P, GATHERS], U32)
        mir = sb("mir", [P, 3])
        own = sb("own", [P, 2])
        notown = sb("notown", [P, 2])
        keep = sb("keep", [P, 4])
        idx = sb("idx", [P, GATHERS], U32)
        rowbase = sb("rowbase", [P, 1], U32)
        rowstep = sb("rowstep", [P, 1], U32)
        val = sb("val", [P, 6])
        nv0 = sb("nv0", [P, 1])
        e6 = sb("e6", [P, 6])
        wsum = sb("wsum", [P, 1])
        rsum = sb("rsum", [P, 2])
        wf = sb("wfac", [P, 2, 8])

        tr = ctx.enter_context(nc.psum_tensor("tr", [P, 2, 512], F32))
        fe = ctx.enter_context(nc.psum_tensor("fe", [P, 2, 512], F32))
        acc = ctx.enter_context(nc.psum_tensor("acc", [P, 2, 512], F32))
        hps = ctx.enter_context(nc.psum_tensor("hps", [P, 512], F32))
        small = ctx.enter_context(nc.psum_tensor("small", [P, 512], F32))

        k_loaded = [sem(f"k_loaded{u}") for u in range(2)]
        base_loaded = [sem(f"base_loaded{u}") for u in range(2)]
        out_stored = [sem(f"out_stored{u}") for u in range(2)]
        up_loaded, up_hi, up_lo = sem("up_loaded"), sem("up_hi"), sem("up_lo")
        const_ready = sem("const_ready")
        base_ready = sem("base_ready")
        names = ("stats1 rstd1 norm1 xn_ready fold_even even_folded fold_odd1 fold_odd t1_done foT_hi foT_lo f_done sq_done "
                 "p_ready t2_done pT_hi pT_lo i_done o_copied corr_done vals_ready wexp_done "
                 "wf_ready acc0_done x2_ready stats2 rstd2 norm2 x2n_ready t3_done xT_hi xT_lo ds_done s_copied "
                 "mean_done smax_done sexp_done hs_ready h_tr hT_hi hT_lo base_done acc_done out_ready").split()
        S = {n: sem(n) for n in names}
        gathered = [sem(f"gathered{s}") for s in range(GATHERS)]
        block = ctx.enter_context(nc.Block())

        FIRST, LOOP = -3, (1, 30)

        def steps(eng, step):
            for i in range(FIRST, 2 * LOOP[0]):
                step(i // 2, i % 2)
            with eng.Fori(LOOP[0], LOOP[1]) as r:
                step(r, 0)
                step(r, 1)
            for i in range(2 * LOOP[1], NT + 1):
                step(i // 2, i % 2)

        def has(r, u, off):
            return not isinstance(r, int) or 0 <= 2 * r + u + off < NT

        def upto(eng, name, r, u, off, per=1):
            sm = S[name]
            if isinstance(r, int):
                if 2 * r + u + off >= 0:
                    eng.wait_ge(sm, per * (2 * r + u + off + 1))
            else:
                eng.wait_ge(sm, r * (2 * per) + per * (u + off + 1))

        def dma_upto(eng, sems, r, u, off):
            p, k = (u + off) % 2, (u + off) // 2
            if isinstance(r, int):
                if r + k >= 0:
                    eng.wait_ge(sems[p], 16 * (r + k + 1))
            else:
                eng.wait_ge(sems[p], r * 16 + 16 * (k + 1))

        @block.sync
        def _(sp):
            sp.dma_start(gb[:, 0:RC, :], up.rearrange("(c p) o -> p c o", p=P)).then_inc(up_loaded, 16)

            def number(r, mult, add):
                return mult * r + add if isinstance(r, int) else sp.snap(r * mult + add)

            def step(r, u):
                t4, t1, tm = ((u + o) % 2 for o in (4, 1, -1))
                row4, row1, rowm = (number(r, 2 * H, (u + o) * H) for o in (4, 1, -1))
                xn_need = number(r, 2, u + 3)
                out_need = number(r, 2, u)
                st_need = number(r, 16, 16 * ((u - 1) // 2 + 1))
                if has(r, u, 4):
                    if not isinstance(r, int) or 2 * r + u + 2 >= 0:
                        sp.wait_ge(S["xn_ready"], xn_need)
                    sp.dma_start(kt[:, t4], by_row[bass.ds(row4, H), 0:L]).then_inc(k_loaded[t4], 16)
                if has(r, u, -1):
                    sp.wait_ge(S["out_ready"], out_need)
                    sp.dma_start(out_rows[bass.ds(rowm, H), :], x2[:, tm]).then_inc(out_stored[tm], 16)
                if has(r, u, 1):
                    if has(r, u, -1):
                        sp.wait_ge(out_stored[tm], st_need)
                    sp.dma_start(x2[:, t1], by_row[bass.ds(row1, H), 0:L]).then_inc(base_loaded[t1], 16)

            sp.dma_start(kt[:, 0], by_row[0:H, 0:L]).then_inc(k_loaded[0], 16)
            steps(sp, step)
            for u in range(2):
                sp.wait_ge(out_stored[u], 16 * NT // 2)

        @block.gpsimd
        def _(pool):
            G = nc.gpsimd
            G.memset(mean_of[:, :], 1.0 / H).then_inc(const_ready, 1)
            G.memset(mhalf[:, :], -0.5).then_inc(const_ready, 1)
            G.iota(rowbase[:, :], [[0, 1]], base=0, channel_multiplier=ROW).then_inc(const_ready, 1)
            G.memset(rowstep[:, :], H * ROW).then_inc(const_ready, 1)
            pool.wait_ge(const_ready, 4)
            pool.wait_ge(up_lo, 1)

            def step(r, u):
                if has(r, u, 3):
                    a = (u + 3) % 2
                    upto(pool, "stats1", r, u, 3)
                    G.tensor_tensor(n1[:, a, 0:1], c1[:, a, 0:1], mhalf[:, :], ALU.pow).then_inc(S["rstd1"], 1)
                    upto(pool, "rstd1", r, u, 3)
                    G.tensor_tensor(n1[:, a, 1:2], c1[:, a, 1:2], n1[:, a, 0:1], ALU.mult).then_inc(S["norm1"], 1)
                if has(r, u, 1):
                    upto(pool, "x2_ready", r, u, 0)
                    upto(pool, "vals_ready", r, u, 1)
                    G.tensor_tensor(idx[:, :], lag[:, :], rowbase[:, :].broadcast_to([P, GATHERS]), ALU.add)
                    pool.drain()
                    G.tensor_tensor(rowbase[:, :], rowbase[:, :], rowstep[:, :], ALU.add)
                    for s in range(GATHERS):
                        G.indirect_dma_start(gb[:, s], None, twice,
                                             bass.IndirectOffsetOnAxis(ap=idx[:, s:s + 1], axis=0)).then_inc(gathered[s], 16)
                if has(r, u, 3):
                    upto(pool, "xn_ready", r, u, 3)
                    G.tensor_tensor(odd[:, 1:HALF], xn[:, 1:HALF], xn[:, L - 1:HALF:-1], ALU.subtract)\
                        .then_inc(S["fold_odd1"], 1)
                    upto(pool, "fold_odd1", r, u, 3)
                    upto(pool, "t1_done", r, u, 1)
                    lo, hi = odd[:, 1:Q + 1], odd[:, HALF - 1:Q - 1:-1]
                    G.tensor_tensor(fo[:, a, 2], lo, hi, ALU.subtract).then_inc(S["fold_odd"], 1)
                    G.tensor_tensor(fo[:, a, 3], lo, hi, ALU.add).then_inc(S["fold_odd"], 1)
                if has(r, u, 2):
                    upto(pool, "t2_done", r, u, 1)
                    upto(pool, "sq_done", r, u, 2)
                    G.tensor_tensor(pw[:, :], sq[:, 0], sq[:, 1], ALU.add).then_inc(S["p_ready"], 1)
                if has(r, u, 1):
                    upto(pool, "stats2", r, u, 1)
                    G.tensor_tensor(n2[:, 0:1], c2[:, 0:1], mhalf[:, :], ALU.pow).then_inc(S["rstd2"], 1)
                    upto(pool, "rstd2", r, u, 1)
                    G.tensor_tensor(n2[:, 1:2], c2[:, 1:2], n2[:, 0:1], ALU.mult).then_inc(S["norm2"], 1)
            steps(pool, step)

        @block.scalar
        def _(act):
            A = nc.scalar.activation
            act.wait_ge(up_loaded, 16)
            A(u16[:, 0], gb[:, 0:RC, :], ACT.Copy, scale=scale[:, 2:3]).then_inc(up_hi, 1)

            def step(r, u):
                if has(r, u, 3):
                    a = (u + 3) % 2
                    upto(act, "norm1", r, u, 3)
                    upto(act, "fold_even", r, u, 2)
                    upto(act, "fold_odd1", r, u, 2)
                    A(xn[:, :], kt[:, a], ACT.Identity, scale=n1[:, a, 0:1], bias=n1[:, a, 1:2]).then_inc(S["xn_ready"], 1)
                if has(r, u, 1):
                    upto(act, "vals_ready", r, u, 1)
                    A(e6[:, :], val[:, :], ACT.Exp, bias=nv0[:, :], accum_out=wsum[:, :]).then_inc(S["wexp_done"], 1)
                if has(r, u, 0):
                    upto(act, "ds_done", r, u, 0)
                    A(sc[:, :], small[:, 0:E], ACT.Copy).then_inc(S["s_copied"], 1)
                if has(r, u, 2):
                    upto(act, "f_done", r, u, 1)
                    upto(act, "t1_done", r, u, 2)
                    A(foT[:, 0].rearrange("p c h -> p (c h)"), tr[:, :, :].rearrange("p a b -> p (a b)"), ACT.Copy)\
                        .then_inc(S["foT_hi"], 1)
                if has(r, u, 0):
                    upto(act, "smax_done", r, u, 0)
                    A(ex8[:, :], small[:, E:2 * E], ACT.Exp, scale=scale[:, 5:6], bias=soft[:, 1:2],
                      accum_out=soft[:, 2:3]).then_inc(S["sexp_done"], 1)
                if has(r, u, 1):
                    t = (u + 1) % 2
                    upto(act, "wf_ready", r, u, 1)
                    dma_upto(act, base_loaded, r, u, 1)
                    A(x2[:, t], x2[:, t], ACT.Identity, scale=wf[:, t, 6:7], bias=wf[:, t, 7:8])\
                        .then_inc(S["acc0_done"], 1)
                if has(r, u, 2):
                    upto(act, "p_ready", r, u, 1)
                    upto(act, "f_done", r, u, 2)
                    A(sq[:, :, :], fe[:, :, :], ACT.Square, scale=1.0 / 32).then_inc(S["sq_done"], 1)
                if has(r, u, 0):
                    upto(act, "acc_done", r, u, -1)
                    upto(act, "h_tr", r, u, 0)
                    A(hT[:, 0].rearrange("p c h -> p (c h)"), tr[:, 1], ACT.Copy).then_inc(S["hT_hi"], 1)
                if has(r, u, 2):
                    upto(act, "i_done", r, u, 1)
                    upto(act, "t2_done", r, u, 2)
                    A(pT[:, 0].rearrange("p c h -> p (c h)"), tr[:, 0], ACT.Copy).then_inc(S["pT_hi"], 1)
                if has(r, u, 1):
                    upto(act, "norm2", r, u, 1)
                    upto(act, "t3_done", r, u, 0)
                    t = (u + 1) % 2
                    A(x2n[:, :], x2[:, t], ACT.Identity, scale=n2[:, 0:1], bias=n2[:, 1:2]).then_inc(S["x2n_ready"], 1)
                if has(r, u, 2):
                    upto(act, "corr_done", r, u, 1)
                    upto(act, "i_done", r, u, 2)
                    A(osb[:, :], fe[:, 1, 0:M], ACT.Copy).then_inc(S["o_copied"], 1)
                if has(r, u, 1):
                    t = (u + 1) % 2
                    upto(act, "base_done", r, u, -1)
                    upto(act, "t3_done", r, u, 1)
                    A(xT[:, t, 0].rearrange("p c h -> p (c h)"), tr[:, :, :].rearrange("p a b -> p (a b)"), ACT.Copy)\
                        .then_inc(S["xT_hi"], 1)
            steps(act, step)

        @block.vector
        def _(dve):
            V = nc.vector

            def ts(out, in0, a, b=None, op0=ALU.mult, op1=ALU.bypass):
                return V.tensor_scalar(out, in0, a, b, op0, op1)

            stt = V.scalar_tensor_tensor
            dve.wait_ge(up_hi, 1)
            stt(u16[:, 1], gb[:, 0:RC, :], scale[:, 2:3], u16[:, 0], ALU.mult, ALU.subtract).then_inc(up_lo, 1)
            dve.wait_ge(const_ready, 4)

            def stats(src, st_, mv_, c_, name):
                V.bn_stats(st_[:, 0:6], src[:, 0:512])
                V.bn_stats(st_[:, 6:12], src[:, 512:1024])
                dve.drain()
                V.bn_aggr(mv_[:, :], st_[:, :])
                dve.drain()
                ts(c_[:, 0:1], mv_[:, 1:2], LN_EPS, None, ALU.add)
                ts(c_[:, 1:2], mv_[:, 0:1], -1.0)
                dve.drain().then_inc(S[name], 1)

            def step(r, u):
                if has(r, u, -1):
                    upto(dve, "acc_done", r, u, -1)
                    t = (u - 1) % 2
                    stt(x2[:, t], acc[:, :, :].rearrange("p a b -> p (a b)"), scale[:, 4:5], x2[:, t],
                        ALU.mult, ALU.add).then_inc(S["out_ready"], 1)
                if has(r, u, 1):
                    V.tensor_copy(nk[:, :], n1[:, (u + 1) % 2])
                    dve.drain()
                if has(r, u, 3):
                    a = (u + 3) % 2
                    dma_upto(dve, k_loaded, r, u, 3)
                    stats(kt[:, a], st, mv, c1[:, a], "stats1")
                if has(r, u, 1):
                    dve.drain()
                    V.max_index(i8[:, :], m8[:, :], cb[:, 1:HALF + 1])
                    dve.drain()
                    ts(lag[:, 0:3], i8[:, 0:3], 1.0, None, ALU.add)
                    ts(mir[:, :], i8[:, 0:3], -1.0, float(L - 1), ALU.mult, ALU.add)
                    ts(own[:, :], i8[:, 0:2], float(HALF - 1), None, ALU.is_equal)
                    dve.drain()
                    ts(notown[:, :], own[:, :], -1.0, 1.0, ALU.mult, ALU.add)
                    dve.drain()
                    V.tensor_tensor(keep[:, 0:2], notown[:, :], mir[:, 0:2], ALU.mult)
                    V.tensor_tensor(keep[:, 2:4], notown[:, :], m8[:, 0:2], ALU.mult)
                    V.tensor_copy(val[:, 0:3], m8[:, 0:3])
                    V.tensor_copy(val[:, 5:6], cb[:, 0:1])
                    ts(nv0[:, :], cb[:, 0:1], -1.0)
                    dve.drain()
                    stt(lag[:, 3:5], own[:, :], mir[:, 2:3], keep[:, 0:2], ALU.mult, ALU.add)
                    stt(val[:, 3:5], own[:, :], m8[:, 2:3], keep[:, 2:4], ALU.mult, ALU.add)
                    dve.drain().then_inc(S["vals_ready"], 1)
                if has(r, u, 2):
                    upto(dve, "foT_hi", r, u, 2)
                    V.tensor_tensor(foT[:, 1].rearrange("p c h -> p (c h)"), tr[:, :, :].rearrange("p a b -> p (a b)"),
                                    foT[:, 0].rearrange("p c h -> p (c h)"), ALU.subtract).then_inc(S["foT_lo"], 1)
                if has(r, u, 0):
                    upto(dve, "mean_done", r, u, 0)
                    V.tensor_reduce(soft[:, 0:1], small[:, E:2 * E], axis=AX, op=ALU.max)
                    dve.drain()
                    ts(soft[:, 1:2], soft[:, 0:1], scale[:, 5:6], -1.0, ALU.mult, ALU.mult).then_inc(S["smax_done"], 1)
                if has(r, u, 1):
                    t = (u + 1) % 2
                    upto(dve, "wexp_done", r, u, 1)
                    V.reciprocal(rsum[:, 0:1], wsum[:, :])
                    dve.drain()
                    V.tensor_tensor(rsum[:, 1:2], rsum[:, 0:1], nk[:, 0:1], ALU.mult)
                    dve.drain()
                    ts(wf[:, t, 0:6], e6[:, :], rsum[:, 1:2])
                    ts(wf[:, t, 6:7], e6[:, 5:6], rsum[:, 1:2], 1.0, ALU.mult, ALU.add)
                    V.tensor_copy(wf[:, t, 7:8], nk[:, 1:2])
                    dve.drain().then_inc(S["wf_ready"], 1)
                if has(r, u, 0):
                    upto(dve, "sexp_done", r, u, 0)
                    V.reciprocal(soft[:, 3:4], soft[:, 2:3])
                    dve.drain()
                    upto(dve, "h_tr", r, u, -1)
                    stt(hs[:, :].rearrange("p (e r) -> p e r", e=E), hps[:, :].rearrange("p (e r) -> p e r", e=E),
                        soft[:, 3:4], ex8[:, :].unsqueeze(2).broadcast_to([P, E, R]), ALU.mult, ALU.mult)\
                        .then_inc(S["hs_ready"], 1)
                if has(r, u, 3):
                    a = (u + 3) % 2
                    upto(dve, "xn_ready", r, u, 3)
                    V.tensor_tensor(evn[:, 1:HALF], xn[:, 1:HALF], xn[:, L - 1:HALF:-1], ALU.add)
                    V.tensor_copy(evn[:, 0:HALF + 1:HALF], xn[:, 0:HALF + 1:HALF])
                    dve.drain().then_inc(S["fold_even"], 1)
                    upto(dve, "t1_done", r, u, 1)
                    lo, hi = evn[:, 0:Q], evn[:, HALF:Q:-1]
                    V.tensor_tensor(fo[:, a, 0], lo, hi, ALU.add)
                    V.tensor_tensor(fo[:, a, 1], lo, hi, ALU.subtract)
                    dve.drain().then_inc(S["even_folded"], 1)
                if has(r, u, 1):
                    t = (u + 1) % 2
                    upto(dve, "acc0_done", r, u, 1)
                    for s in range(GATHERS):
                        if isinstance(r, int):
                            dve.wait_ge(gathered[s], 16 * (2 * r + u + 2))
                        else:
                            dve.wait_ge(gathered[s], r * 32 + 16 * (u + 2))
                        last = stt(x2[:, t], gb[:, s], wf[:, t, s:s + 1], x2[:, t], ALU.mult, ALU.add)
                        if s < GATHERS - 1:
                            dve.drain()
                    last.then_inc(S["x2_ready"], 1)
                if has(r, u, 0):
                    upto(dve, "hT_hi", r, u, 0)
                    V.tensor_tensor(hT[:, 1].rearrange("p c h -> p (c h)"), tr[:, 1],
                                    hT[:, 0].rearrange("p c h -> p (c h)"), ALU.subtract).then_inc(S["hT_lo"], 1)
                if has(r, u, 2):
                    upto(dve, "pT_hi", r, u, 2)
                    V.tensor_tensor(pT[:, 1].rearrange("p c h -> p (c h)"), tr[:, 0],
                                    pT[:, 0].rearrange("p c h -> p (c h)"), ALU.subtract).then_inc(S["pT_lo"], 1)
                if has(r, u, 1):
                    dve.drain()
                    stats(x2[:, (u + 1) % 2], st2, mv2, c2, "stats2")
                if has(r, u, 2):
                    upto(dve, "o_copied", r, u, 2)
                    V.tensor_tensor(cb[:, 0:M], fe[:, 0, 0:M], osb[:, :], ALU.add)
                    V.tensor_tensor(cb[:, HALF:Q:-1], fe[:, 0, 0:Q], osb[:, 0:Q], ALU.subtract)
                    dve.drain().then_inc(S["corr_done"], 1)
                    V.max(m8[:, :], cb[:, 1:HALF + 1])
                if has(r, u, 1):
                    t = (u + 1) % 2
                    upto(dve, "xT_hi", r, u, 1)
                    V.tensor_tensor(xT[:, t, 1].rearrange("p c h -> p (c h)"), tr[:, :, :].rearrange("p a b -> p (a b)"),
                                    xT[:, t, 0].rearrange("p c h -> p (c h)"), ALU.subtract).then_inc(S["xT_lo"], 1)
            steps(dve, step)

        @block.tensor
        def _(pe):
            mm = nc.tensor.matmul
            PASSES = ((0, 0), (0, 1), (1, 0))

            def down_and_scores(x):
                for c in range(IC):
                    for a, b in PASSES:
                        first, last = c == 0 and (a, b) == (0, 0), c == IC - 1 and a == 1
                        mm(hps[:, :], x[:, a, c], d16[:, b, c], start=first, stop=last)
                        m = mm(small[:, 0:E], x[:, a, c], kq16[:, b, c], start=first, stop=last)
                return m

            def base(x, chunks):
                for c in chunks:
                    for a, b in PASSES:
                        for o in range(2):
                            m = mm(acc[:, o], x[:, a, c], w16[:, b, c, o * 512:(o + 1) * 512],
                                   start=c == 0 and (a, b) == (0, 0), stop=False, skip_group_check=True)
                return m

            def lora_up(chunks):
                for c in chunks:
                    for a, b in PASSES:
                        for o in range(2):
                            m = mm(acc[:, o], hT[:, a, c], u16[:, b, c, o * 512:(o + 1) * 512],
                                   start=False, stop=c == RC - 1 and a == 1, skip_group_check=True)
                return m

            def forward():
                for part in range(4):
                    for c in range(2):
                        for a, b in PASSES:
                            m = mm(fe[:, part // 2, (part % 2) * Q:(part % 2 + 1) * Q], foT[:, a, 2 * part + c],
                                   fwd[:, b, 2 * part + c], start=c == 0 and (a, b) == (0, 0), stop=c == 1 and a == 1)
                return m

            def backward():
                for part in range(2):
                    for c in range(2):
                        for a, b in PASSES:
                            m = mm(fe[:, part, 0:MS], pT[:, a, 2 * part + c], inv[:, b, 2 * part + c],
                                   start=c == 0 and (a, b) == (0, 0), stop=c == 1 and a == 1)
                return m

            def transposes(dst, src, count):
                for c in range(count):
                    m = nc.tensor.transpose(dst[:, c * P:(c + 1) * P], src[:, c * P:(c + 1) * P], ident[:, :])
                return m

            tr_flat = tr[:, :, :].rearrange("p a b -> p (a b)")
            pe.wait_ge(const_ready, 4)

            def step(r, u):
                x = xT[:, u]
                if has(r, u, 0):
                    upto(pe, "xT_lo", r, u, 0)
                    upto(pe, "hs_ready", r, u, -1)
                    down_and_scores(x).then_inc(S["ds_done"], 1)
                if has(r, u, 2):
                    a = (u + 2) % 2
                    upto(pe, "fold_odd", r, u, 2, 2)
                    upto(pe, "even_folded", r, u, 2)
                    upto(pe, "xT_lo", r, u, 0)
                    transposes(tr_flat, fo[:, a].rearrange("p a b -> p (a b)"), 8).then_inc(S["t1_done"], 1)
                if has(r, u, 0):
                    upto(pe, "s_copied", r, u, 0)
                    mm(small[:, E:2 * E], mean_of[:, :], sc[:, :], start=True, stop=True).then_inc(S["mean_done"], 1)
                    upto(pe, "out_ready", r, u, -1)
                    base(x, range(0, 3))
                if has(r, u, 2):
                    upto(pe, "foT_lo", r, u, 2)
                    upto(pe, "corr_done", r, u, 1)
                    forward().then_inc(S["f_done"], 1)
                if has(r, u, 0):
                    base(x, range(3, 5))
                    upto(pe, "hs_ready", r, u, 0)
                    if has(r, u, 2):
                        upto(pe, "foT_lo", r, u, 2)
                    transposes(tr[:, 1], hs[:, :], RC).then_inc(S["h_tr"], 1)
                if has(r, u, 2):
                    upto(pe, "p_ready", r, u, 2)
                    transposes(tr[:, 0], pw[:, :], 4).then_inc(S["t2_done"], 1)
                if has(r, u, 0):
                    base(x, range(5, IC)).then_inc(S["base_done"], 1)
                if has(r, u, 2):
                    upto(pe, "pT_lo", r, u, 2)
                    upto(pe, "sq_done", r, u, 2)
                    backward().then_inc(S["i_done"], 1)
                if has(r, u, 0):
                    upto(pe, "hT_lo", r, u, 0)
                    lora_up(range(0, RC // 2))
                if has(r, u, 1):
                    upto(pe, "x2n_ready", r, u, 1)
                    if has(r, u, 2):
                        upto(pe, "pT_lo", r, u, 2)
                    if has(r, u, 0):
                        upto(pe, "hT_lo", r, u, 0)
                    transposes(tr_flat, x2n[:, :], 8).then_inc(S["t3_done"], 1)
                if has(r, u, 0):
                    lora_up(range(RC // 2, RC)).then_inc(S["acc_done"], 1)
            steps(pe, step)


def kernel(**inputs):
    import concourse.bacc as bacc
    from concourse.bass_utils import run_bass_kernel_spmd

    x = inputs["x"]
    part = np.transpose(x, (3, 2, 1, 0))
    fwd_c, inv_c = dft_constants()
    down = np.transpose(inputs["L0_ffn_lora_down"], (1, 0, 2)).reshape(L, ER)
    arrays = {
        "w_re": np.concatenate([part[0], part[0]]), "w_im": np.concatenate([part[1], part[1]]),
        "log_dt": inputs["L0_tok_log_dt"].T,
        "lam": np.concatenate([inputs["L0_tok_Lambda"]] * 2),
        "w_org": inputs["L0_ffn_W_org"].T, "down": down,
        "up": inputs["L0_ffn_lora_up"].reshape(ER, L), "keys": inputs["L0_ffn_lora_keys"].T,
        "wq": inputs["L0_ffn_Wq"],
        "fwd": fwd_c, "inv": inv_c, "eye": np.eye(P, dtype=np.float32),
    }
    arrays = {k: np.ascontiguousarray(a) for k, a in arrays.items()}
    nc = bacc.Bacc("TRN2", target_bir_lowering=False, num_devices=1)
    args = [nc.dram_tensor(f"in_{k}", a.shape, mybir.dt.from_np(a.dtype), kind="ExternalInput").ap()
            for k, a in arrays.items()]
    out = nc.dram_tensor("out", (NT, H, L), F32, kind="ExternalOutput").ap()
    vit_tower(nc, *args, out)
    r = run_bass_kernel_spmd(nc, [{f"in_{k}": a for k, a in arrays.items()}], core_ids=[0])
    return r.results[0]["out"]
```

```python
from contextlib import ExitStack

import numpy as np

import concourse.bass as bass
from concourse import mybir

F32 = mybir.dt.float32
F16 = mybir.dt.float16
U32 = mybir.dt.uint32
I32 = mybir.dt.int32
ALU = mybir.AluOpType
ACT = mybir.ActivationFunctionType
AX = mybir.AxisListType.X

P = 128
NT = 64
H = 128
N = 64
L = 1024
HALF = L // 2
PARTS = 4
PART = L // PARTS
E, R, KEY = 8, 64, 128
ER = E * R
IC = L // P
RC = ER // P
WH = IC // 2
Q = 256
M = 257
MS = 258
ROW = 2 * L
LN_EPS = 1e-5
REC_EPS = 1e-7
TOP = 2.0 ** 13
DOWN_TOP = 2.0 ** 9
ROUND = 12582912.0
TURN = 6.283185
SCORE = KEY ** -0.5
HB = 8
NB = H // HB
GATHERS = 5
GROW, SIGN, PHASE, SHIFT = range(4)


def split16(a):
    hi = a.astype(np.float16)
    return hi, (a - hi.astype(np.float64)).astype(np.float16)


def dft_constants():
    w = 2 * np.pi / L
    l0, l1 = np.arange(Q)[:, None], np.arange(1, Q + 1)[:, None]
    even, odd = 2 * np.arange(Q)[None] + 2, 2 * np.arange(Q)[None] + 1
    re_even = np.cos(w * (l0 * even % L)) - np.cos(w * (Q * even % L))
    re_odd = np.cos(w * (l0 * odd % L))
    im_even = np.sin(w * (l1 * even % L))
    im_odd = np.sin(w * (l1 * odd % L))
    im_odd[-1] *= 0.5
    fwd = np.concatenate([re_even, re_odd, im_even, im_odd]).reshape(8, P, Q).transpose(1, 0, 2)
    m = np.arange(M)[None]
    weight = np.where(even.T == HALF, 1.0, 2.0)
    inv = np.concatenate([weight * np.cos(w * (even.T * m % L)), 2 * np.cos(w * (odd.T * m % L))])
    inv = np.pad(inv, ((0, 0), (0, MS - M))).reshape(4, P, MS).transpose(1, 0, 2)
    return np.stack(split16(fwd), 1), np.stack(split16(inv), 1)


def vit_tower(nc, wre, wim, log_dt, lam, w_org, down, up, keys, wq, fwd_c, inv_c, eye, out):
    with ExitStack() as ctx:
        def sb(name, shape, dt=F32):
            return ctx.enter_context(nc.sbuf_tensor(name, shape, dt))

        k_rows = nc.dram_tensor("k_rows", (NT * H, L), F32, kind="Internal").ap()
        by_half = k_rows.rearrange("(c h) (a b) -> a c h b", c=NT, a=2)
        out_rows = out.rearrange("c h l -> (c h) l")

        ident = sb("ident", [P, P])
        w16 = sb("w16", [P, 2, IC, L], F16)
        d16 = sb("d16", [P, 2, IC, ER], F16)
        kq = sb("kq", [P, IC, E])
        fwd = sb("fwd", [P, 2, 8, Q], F16)
        inv = sb("inv", [P, 2, 4, MS], F16)
        scale = sb("scale", [P, 4])
        zr = sb("zr", [P, H])
        turns = sb("turns", [P, H])
        s1 = sb("s1", [P, PARTS, H])
        s2 = sb("s2", [P, PARTS, H])
        pos = sb("pos", [P, PART])
        side = sb("side", [P, SHIFT + PARTS])
        half = sb("half", [P, WH, L])
        half_loaded = ctx.enter_context(nc.semaphore("half_loaded"))

        tables(nc, locals())
        generate(nc, locals())
        tower(nc, locals())


def tables(nc, v):
    ident, kq, fwd, inv, scale = (v[k] for k in ("ident", "kq", "fwd", "inv", "scale"))
    half, half_loaded = v["half"], v["half_loaded"]
    zr, turns, s1, s2, pos, side = (v[k] for k in ("zr", "turns", "s1", "s2", "pos", "side"))
    w_chunks = v["w_org"].rearrange("(c p) o -> p c o", p=P)
    down, up, keys, wq, log_dt, lam = (v[k] for k in ("down", "up", "keys", "wq", "log_dt", "lam"))
    with ExitStack() as ctx:
        def sb(name, shape, dt=F32):
            return ctx.enter_context(nc.sbuf_tensor(name, shape, dt))

        def sem(name):
            return ctx.enter_context(nc.semaphore(name))

        wf = sb("wf", [P, IC, L])
        df = sb("df", [P, IC, ER])
        uf = sb("uf", [P, RC, L])
        wqf = sb("wqf", [P, L])
        keysf = sb("keysf", [P, E])
        ones = sb("ones", [P, P])
        sums = sb("sums", [P, 3])
        total = sb("total", [P, 3])
        root = sb("root", [P, 3])
        one_half = sb("one_half", [P, 3])
        power = sb("power", [P, 3])
        limit = sb("limit", [P, 4])
        lamf = sb("lamf", [P, 2])
        dt = sb("dt", [P, 2, H])
        z = sb("z", [P, 2, H])
        zneg = sb("zneg", [P, 2, H])
        tin = sb("tin", [P, 2, H])
        th = sb("th", [P, 2, H])
        ein = sb("ein", [P, PARTS, H])
        ex = sb("ex", [P, PARTS, H])
        ang = sb("ang", [P, 4 + 2 * PARTS, H])
        whole = sb("whole", [P, 4 + 2 * PARTS, H])
        sn = sb("sn", [P, 4 + 2 * PARTS, H])
        rot = sb("rot", [P, 2, PARTS, H])
        wk = [sb(f"wk{i}", [P, 2, H]) for i in range(6)]
        re, im = sb("re", [P, 2, H]), sb("im", [P, 2, H])
        q = [sb(f"q{i}", [P, H]) for i in range(10)]
        prod = sb("prod", [P, 4, PARTS, H])
        ps_kq = ctx.enter_context(nc.psum_tensor("ps_kq", [P, IC * E], F32))
        ps_sums = ctx.enter_context(nc.psum_tensor("ps_sums", [P, 3], F32))

        w_loaded, down_loaded, up_loaded = sem("w_loaded"), sem("down_loaded"), sem("up_loaded")
        const_loaded = sem("const_loaded")
        wq_loaded = sem("wq_loaded")
        kq_done = sem("kq_done")
        fills_ready = sem("fills_ready")
        sums_ready = sem("sums_ready")
        total_ready = sem("total_ready")
        total_copied = sem("total_copied")
        root_ready = sem("root_ready")
        small_loaded = sem("small_loaded")
        dt_ready = sem("dt_ready")
        args_ready = sem("args_ready")
        funcs_ready = sem("funcs_ready")
        pos_ready = sem("pos_ready")
        block = ctx.enter_context(nc.Block())

        @block.sync
        def _(sp):
            sp.dma_start(dt[:, 0, :], log_dt[0:1, :].partition_broadcast(P)).then_inc(small_loaded, 16)
            sp.dma_start(dt[:, 1, :], log_dt[1:2, :].partition_broadcast(P)).then_inc(small_loaded, 16)
            sp.dma_start(lamf[:, :], lam).then_inc(small_loaded, 16)
            sp.dma_start(wqf[:, :], wq).then_inc(wq_loaded, 16)
            sp.dma_start(keysf[:, :], keys).then_inc(wq_loaded, 16)
            sp.dma_start(wf[:, :, :], w_chunks).then_inc(w_loaded, 16)
            sp.dma_start(df[:, :, :], down.rearrange("(c p) o -> p c o", p=P)).then_inc(down_loaded, 16)
            sp.dma_start(uf[:, :, :], up.rearrange("(c p) o -> p c o", p=P)).then_inc(up_loaded, 16)
            sp.dma_start(ident[:, :], v["eye"]).then_inc(const_loaded, 16)
            sp.dma_start(fwd[:, :, :, :], v["fwd_c"]).then_inc(const_loaded, 16)
            sp.dma_start(inv[:, :, :, :], v["inv_c"]).then_inc(const_loaded, 16)
            sp.dma_start(half[:, :, :], w_chunks[:, 0:WH]).then_inc(half_loaded, 16)
            sp.wait_ge(const_loaded, 48)

        @block.tensor
        def _(pe):
            pe.wait_ge(wq_loaded, 32)
            for c in range(IC):
                last = nc.tensor.matmul(ps_kq[:, c * E:(c + 1) * E], wqf[:, c * P:(c + 1) * P], keysf[:, :],
                                        start=True, stop=True)
            last.then_inc(kq_done, 1)
            pe.wait_ge(fills_ready, 2)
            pe.wait_ge(sums_ready, 3)
            nc.tensor.matmul(ps_sums[:, :], ones[:, :], sums[:, :], start=True, stop=True).then_inc(total_ready, 1)

        @block.gpsimd
        def _(pool):
            nc.gpsimd.iota(pos[:, :], [[1, PART]], base=0, channel_multiplier=0,
                           allow_small_or_imprecise_dtypes=True).then_inc(pos_ready, 1)
            nc.gpsimd.memset(ones[:, :], 1.0).then_inc(fills_ready, 1)
            nc.gpsimd.memset(one_half[:, :], 0.5).then_inc(fills_ready, 1)
            pool.wait_ge(fills_ready, 2)
            pool.wait_ge(total_copied, 1)
            nc.gpsimd.tensor_tensor(root[:, :], total[:, :], one_half[:, :], ALU.pow).then_inc(root_ready, 1)

        @block.scalar
        def _(act):
            act.wait_ge(small_loaded, 48)
            nc.scalar.activation(dt[:, :, :], dt[:, :, :], ACT.Exp).then_inc(dt_ready, 1)
            act.wait_ge(args_ready, 1)
            nc.scalar.activation(th[:, :, :], tin[:, :, :], ACT.Tanh).then_inc(funcs_ready, 1)
            nc.scalar.activation(ex[:, :, :], ein[:, :, :], ACT.Exp).then_inc(funcs_ready, 1)
            nc.scalar.activation(sn[:, :, :], ang[:, :, :], ACT.Sin, scale=TURN).then_inc(funcs_ready, 1)
            act.wait_ge(kq_done, 1)
            nc.scalar.activation(kq[:, :, :], ps_kq[:, :].rearrange("p (c e) -> p c e", e=E), ACT.Copy)
            for k, (t, arrived) in enumerate(((wf, w_loaded), (df, down_loaded), (uf, up_loaded))):
                flat = t[:, :, :].rearrange("p a b -> p (a b)")
                act.wait_ge(arrived, 16)
                nc.scalar.activation(flat, flat, ACT.Square, accum_out=sums[:, k:k + 1]).then_inc(sums_ready, 1)

        @block.vector
        def _(dve):
            V = nc.vector

            def ts(out, in0, a, b=None, op0=ALU.mult, op1=ALU.bypass):
                return V.tensor_scalar(out, in0, a, b, op0, op1)

            V.memset(side[:, :], 0.0)
            dve.drain()
            V.memset(side[0:N, PHASE:PHASE + 1], 0.25)
            dve.wait_ge(small_loaded, 48)
            ts(side[:, GROW:GROW + 1], lamf[:, 0:1], 0.0, None, ALU.is_gt)
            dve.drain()
            ts(side[:, SIGN:SIGN + 1], side[:, GROW:GROW + 1], -2.0, 1.0, ALU.mult, ALU.add)
            for a in range(PARTS):
                ts(side[:, SHIFT + a:SHIFT + a + 1], side[:, GROW:GROW + 1], -float(L - PART), float(PART * a),
                   ALU.mult, ALU.add)
            dve.wait_ge(pos_ready, 1)
            ts(power[:, 0:1], side[:, GROW:GROW + 1], -float(PART - 1))
            dve.drain()
            ts(pos[:, :], pos[:, :], power[:, 0:1], None, ALU.add)

            dve.wait_ge(dt_ready, 1)
            for k in range(2):
                ts(z[:, k], dt[:, k], lamf[:, k:k + 1])
            dve.drain()
            ts(zneg[:, :, :], z[:, :, :], side[:, SIGN:SIGN + 1])
            V.tensor_copy(zr[:, :], z[:, 0])
            ts(turns[:, :], z[:, 1], 1.0 / (2 * np.pi))
            dve.drain()
            for k, times in enumerate((1, L)):
                ts(tin[:, k], zneg[:, 0], 0.5 * times)
                ts(ang[:, 2 * k], zneg[:, 1], times / (4 * np.pi))
                ts(ang[:, 2 * k + 1], zneg[:, 1], times / (4 * np.pi), 0.25, ALU.mult, ALU.add)
            for a in range(PARTS):
                f = side[:, SHIFT + a:SHIFT + a + 1]
                ts(ein[:, a], z[:, 0], f)
                ts(ang[:, 4 + 2 * a], turns[:, :], f)
                ts(ang[:, 5 + 2 * a], turns[:, :], f, 0.25, ALU.mult, ALU.add)
            dve.drain()
            ts(whole[:, :, :], ang[:, :, :], ROUND, -ROUND, ALU.add, ALU.add)
            dve.drain()
            V.tensor_tensor(ang[:, :, :], ang[:, :, :], whole[:, :, :], ALU.subtract)
            dve.drain().then_inc(args_ready, 1)

            dve.wait_ge(funcs_ready, 3)
            sin_half, cos_half = sn[:, 0:4:2], sn[:, 1:4:2]
            ts(wk[0][:, :, :], th[:, :, :], -1.0, 1.0, ALU.mult, ALU.add)
            V.scalar_tensor_tensor(wk[2][:, :, :], sin_half, -2.0, sin_half, ALU.mult, ALU.mult)
            V.scalar_tensor_tensor(wk[3][:, :, :], sin_half, 2.0, cos_half, ALU.mult, ALU.mult)
            dve.drain()
            V.reciprocal(wk[1][:, :, :], wk[0][:, :, :])
            dve.drain()
            V.scalar_tensor_tensor(wk[4][:, :, :], th[:, :, :], 2.0, wk[1][:, :, :], ALU.mult, ALU.mult)
            dve.drain()
            V.scalar_tensor_tensor(wk[5][:, :, :], wk[2][:, :, :], 1.0, wk[4][:, :, :], ALU.add, ALU.mult)
            V.scalar_tensor_tensor(im[:, :, :], wk[4][:, :, :], 1.0, wk[3][:, :, :], ALU.add, ALU.mult)
            dve.drain()
            V.tensor_tensor(re[:, :, :], wk[5][:, :, :], wk[2][:, :, :], ALU.add)
            dve.drain()
            lr, li = lamf[:, 0:1], lamf[:, 1:2]
            ts(q[0][:, :], im[:, 1], li)
            ts(q[1][:, :], im[:, 1], lr)
            dve.drain()
            V.scalar_tensor_tensor(q[2][:, :], re[:, 1], lr, q[0][:, :], ALU.mult, ALU.subtract)
            V.scalar_tensor_tensor(q[3][:, :], re[:, 1], li, q[1][:, :], ALU.mult, ALU.add)
            dve.drain()
            V.tensor_tensor(q[4][:, :], q[2][:, :], q[2][:, :], ALU.mult)
            V.tensor_tensor(q[5][:, :], q[3][:, :], q[3][:, :], ALU.mult)
            V.tensor_tensor(q[6][:, :], re[:, 0], q[2][:, :], ALU.mult)
            V.tensor_tensor(q[7][:, :], im[:, 0], q[3][:, :], ALU.mult)
            V.tensor_tensor(q[8][:, :], im[:, 0], q[2][:, :], ALU.mult)
            V.tensor_tensor(q[9][:, :], re[:, 0], q[3][:, :], ALU.mult)
            dve.drain()
            V.scalar_tensor_tensor(q[0][:, :], q[4][:, :], REC_EPS, q[5][:, :], ALU.add, ALU.add)
            dve.drain()
            V.reciprocal(q[1][:, :], q[0][:, :])
            V.tensor_tensor(q[2][:, :], q[6][:, :], q[7][:, :], ALU.add)
            V.tensor_tensor(q[3][:, :], q[8][:, :], q[9][:, :], ALU.subtract)
            dve.drain()
            V.tensor_tensor(q[4][:, :], q[2][:, :], q[1][:, :], ALU.mult)
            V.tensor_tensor(q[5][:, :], q[3][:, :], q[1][:, :], ALU.mult)
            V.tensor_tensor(rot[:, 0], ex[:, :, :], sn[:, 5:4 + 2 * PARTS:2], ALU.mult)
            V.tensor_tensor(rot[:, 1], ex[:, :, :], sn[:, 4:4 + 2 * PARTS:2], ALU.mult)
            dve.drain()
            for k, (part, turn) in enumerate(((4, 0), (5, 1), (4, 1), (5, 0))):
                V.tensor_tensor(prod[:, k], q[part][:, :].unsqueeze(1).broadcast_to([P, PARTS, H]), rot[:, turn],
                                ALU.mult)
            dve.drain()
            low, upp = slice(0, N), slice(N, P)
            V.tensor_tensor(s1[low], prod[low, 0], prod[low, 1], ALU.subtract)
            V.tensor_tensor(s2[upp], prod[upp, 1], prod[upp, 0], ALU.subtract)
            V.scalar_tensor_tensor(s1[upp], prod[upp, 2], -1.0, prod[upp, 3], ALU.mult, ALU.subtract)
            V.scalar_tensor_tensor(s2[low], prod[low, 2], -1.0, prod[low, 3], ALU.mult, ALU.subtract)

            dve.wait_ge(total_ready, 1)
            ts(total[:, :], ps_sums[:, :], 2.0 ** -80, None, ALU.max).then_inc(total_copied, 1)
            dve.wait_ge(root_ready, 1)
            V.tensor_scalar(power[:, :].bitcast(I32), root[:, :].bitcast(I32), 0x7F800000, None, ALU.bitwise_and)
            dve.drain()
            V.reciprocal(limit[:, 0:3], power[:, :])
            dve.drain()
            ts(scale[:, 1:2], limit[:, 1:2], DOWN_TOP)
            ts(limit[:, 3:4], limit[:, 0:1], TOP)
            dve.drain()
            V.scalar_tensor_tensor(scale[:, 2:3], limit[:, 2:3], TOP, scale[:, 1:2], ALU.mult, ALU.mult)
            dve.drain()
            V.tensor_tensor(scale[:, 0:1], limit[:, 3:4], scale[:, 2:3], ALU.min)
            dve.drain()
            V.scalar_tensor_tensor(scale[:, 2:3], scale[:, 0:1], 1.0 / DOWN_TOP, power[:, 1:2], ALU.mult, ALU.mult)
            V.reciprocal(scale[:, 3:4], scale[:, 0:1])


def generate(nc, v):
    zr, turns, s1, s2, pos, side = (v[k] for k in ("zr", "turns", "s1", "s2", "pos", "side"))
    wre, wim, by_half = v["wre"], v["wim"], v["by_half"]
    w16, scale, half, half_loaded = v["w16"], v["scale"], v["half"], v["half_loaded"]
    HG = HB // 2
    with ExitStack() as ctx:
        def sb(name, shape, dt=F32):
            return ctx.enter_context(nc.sbuf_tensor(name, shape, dt))

        def sem(name):
            return ctx.enter_context(nc.semaphore(name))

        wa = sb("wa", [P, 2, HB, N])
        wb = sb("wb", [P, 2, HB, N])
        pr = sb("pr", [P, HB, 2, 2, N])
        wp = sb("wp", [P, 2, HB, 2, 2, N])
        zrb = sb("zrb", [P, 2, HB])
        tub = sb("tub", [P, 2, HB])
        ang = sb("angle", [P, 2, HB, PART])
        whole = sb("whole_turns", [P, HB, PART])
        amp = sb("amp", [P, 2, HB, PART])
        wav = sb("wav", [P, 2, HB, PART])
        kst = sb("kst", [P, 2, HG, HALF])
        ps = ctx.enter_context(nc.psum_tensor("ps_k", [P, HB, HALF], F32))

        w_loaded = [sem(f"w_loaded{u}") for u in range(2)]
        par_ready = sem("par_ready")
        exp_done = sem("exp_done")
        whole_ready = sem("whole_ready")
        part_ready = sem("part_ready")
        sin_done = sem("sin_done")
        wave_ready = sem("wave_ready")
        pr_ready = sem("pr_ready")
        wp_ready = sem("wp_ready")
        k_done = sem("k_done")
        copied = sem("copied")
        stored = [sem(f"stored{g}") for g in range(2)]
        w_hi = sem("w_hi")
        block = ctx.enter_context(nc.Block())

        def blocks(eng, body):
            body(0, 0)
            body(0, 1)
            with eng.Fori(1, NB // 2) as r:
                body(r, 0)
                body(r, 1)

        def has(r, u, off):
            return not isinstance(r, int) or 2 * r + u + off >= 0

        def upto(eng, sm, r, u, off, per=1, short=0):
            if isinstance(r, int):
                if 2 * r + u + off >= 0:
                    eng.wait_ge(sm, per * (2 * r + u + off + 1) - short)
            else:
                eng.wait_ge(sm, r * (2 * per) + per * (u + off + 1) - short)

        def rows_of(r, u):
            b = (2 * r + u) * HB if isinstance(r, int) else r * (2 * HB) + u * HB
            return bass.ds(b, HB)

        def factor(t, r, u, a):
            return t[:, a, rows_of(r, u)].unsqueeze(2).broadcast_to([P, HB, N])

        @block.sync
        def _(sp):
            def load_next(r, u):
                static = isinstance(r, int)
                h2 = (2 * r + u + 2) * HB if static else sp.snap(r * (2 * HB) + (u + 2) * HB)
                need = 2 * r + u + 1 if static else sp.snap(r * 2 + (u + 1))
                for w_s, src in ((wa, wre), (wb, wim)):
                    sp.wait_ge(wp_ready, need)
                    sp.dma_start(w_s[:, u], src[:, bass.ds(h2, HB), :]).then_inc(w_loaded[u], 16)

            def store(r, u, off):
                def number(per, add):
                    add += (u + off) * per
                    return 2 * r * per + add if isinstance(r, int) else sp.snap(r * (2 * per) + add)

                rows = [number(HB, g * HG) for g in range(2)]
                need = [number(2, g + 1) for g in range(2)]
                for g in range(2):
                    for a in range(2):
                        sp.wait_ge(copied, need[g])
                        sp.dma_start(by_half[a, :, bass.ds(rows[g], HG), :],
                                     kst[a * N:(a + 1) * N, g]).then_inc(stored[g], 16)

            for u in range(2):
                for w_s, src in ((wa, wre), (wb, wim)):
                    sp.dma_start(w_s[:, u], src[:, u * HB:(u + 1) * HB, :]).then_inc(w_loaded[u], 16)
            for u in range(2):
                load_next(0, u)
            with sp.Fori(1, NB // 2 - 1) as r:
                for u in range(2):
                    load_next(r, u)
                    store(r, u, -2)
            for b in range(NB - 4, NB):
                store(b // 2, b % 2, 0)
            for g in range(2):
                sp.wait_ge(stored[g], 32 * NB)

        @block.gpsimd
        def _(pool):
            def body(r, u):
                upto(pool, wp_ready, r, u, -1)
                pool.wait_ge(w_loaded[u], 32 * (r + 1) if isinstance(r, int) else r * 32 + 32)
                for a in range(PARTS):
                    nc.gpsimd.tensor_tensor(pr[:, :, a % 2, a // 2], wb[:, u], factor(s2, r, u, a), ALU.mult)\
                        .then_inc(pr_ready, 1)
                upto(pool, whole_ready, r, u, 0)
                nc.gpsimd.tensor_tensor(ang[:, u], ang[:, u], whole[:, :, :], ALU.subtract).then_inc(part_ready, 1)
            blocks(pool, body)

        @block.scalar
        def _(act):
            def copies(r, u, off):
                for g in range(2):
                    upto(act, k_done, r, u, off, 2, 1 - g)
                    upto(act, stored[g], r, u, off - 1, 32)
                    nc.scalar.activation(kst[:, g], ps[:, g * HG:(g + 1) * HG], ACT.Copy).then_inc(copied, 1)

            def body(r, u):
                upto(act, par_ready, r, u, 0)
                upto(act, wave_ready, r, u, -2)
                for j in range(HB):
                    last = nc.scalar.activation(amp[:, u, j], pos[:, :], ACT.Exp, scale=zrb[:, u, j:j + 1])
                last.then_inc(exp_done, 1)
                if has(r, u, -2):
                    copies(r, u, -2)
                upto(act, part_ready, r, u, 0)
                nc.scalar.activation(ang[:, u], ang[:, u], ACT.Sin, scale=TURN).then_inc(sin_done, 1)
            blocks(act, body)
            copies(NB // 2, 0, -2)
            act.wait_ge(half_loaded, 16)
            for c in range(WH):
                nc.scalar.activation(w16[:, 0, c], half[:, c], ACT.Copy, scale=scale[:, 0:1]).then_inc(w_hi, 1)
            copies(NB // 2, 0, -1)

        @block.vector
        def _(dve):
            V = nc.vector

            def angles(r, u):
                upto(dve, exp_done, r, u, -2)
                V.tensor_copy(zrb[:, u], zr[:, rows_of(r, u)])
                V.tensor_copy(tub[:, u], turns[:, rows_of(r, u)])
                dve.drain().then_inc(par_ready, 1)
                for j in range(HB):
                    V.tensor_scalar(ang[:, u, j], pos[:, :], tub[:, u, j:j + 1], side[:, PHASE:PHASE + 1],
                                    ALU.mult, ALU.add)
                dve.drain()
                upto(dve, part_ready, r, u, -1)
                V.tensor_scalar(whole[:, :, :], ang[:, u], ROUND, -ROUND, ALU.add, ALU.add).then_inc(whole_ready, 1)

            def wave(r, u, off):
                w = (u + off) % 2
                upto(dve, k_done, r, u, off - 2, 2)
                upto(dve, exp_done, r, u, off)
                upto(dve, sin_done, r, u, off)
                V.tensor_tensor(wav[:, w], amp[:, w], ang[:, w], ALU.mult).then_inc(wave_ready, 1)

            def stationary(r, u):
                dve.wait_ge(w_loaded[u], 32 * (r + 1) if isinstance(r, int) else r * 32 + 32)
                upto(dve, k_done, r, u, -2, 2)
                for a in range(PARTS):
                    V.tensor_tensor(wp[:, u, :, a % 2, a // 2], wa[:, u], factor(s1, r, u, a), ALU.mult)
                dve.drain()
                upto(dve, pr_ready, r, u, 0, PARTS)
                V.tensor_tensor(wp[:, u], wp[:, u], pr[:, :], ALU.add).then_inc(wp_ready, 1)

            def body(r, u):
                angles(r, u)
                if has(r, u, -1):
                    wave(r, u, -1)
                stationary(r, u)
            blocks(dve, body)
            wave(NB // 2, 0, -1)
            for c in range(WH):
                dve.wait_ge(w_hi, c + 1)
                V.scalar_tensor_tensor(w16[:, 1, c], half[:, c], scale[:, 0:1], w16[:, 0, c], ALU.mult, ALU.subtract)

        @block.tensor
        def _(pe):
            def body(r, u):
                upto(pe, wp_ready, r, u, 0)
                upto(pe, wave_ready, r, u, 0)
                for j in range(HB):
                    if j % HG == 0:
                        upto(pe, copied, r, u, -1, 2, 1 - j // HG)
                    for q in range(2):
                        last = nc.tensor.matmul(ps[:, j, q * PART:(q + 1) * PART],
                                                wp[:, u, j, q].rearrange("p a c -> p (a c)"), wav[:, u, j],
                                                start=True, stop=True)
                    if j % HG == HG - 1:
                        last.then_inc(k_done, 1)
            blocks(pe, body)


def tower(nc, v):
    ident, w16, d16, kq, fwd, inv, scale = (v[k] for k in ("ident", "w16", "d16", "kq", "fwd", "inv", "scale"))
    k_rows, out_rows, down, up = v["k_rows"], v["out_rows"], v["down"], v["up"]
    half, half_loaded = v["half"], v["half_loaded"]
    w_chunks = v["w_org"].rearrange("(c p) o -> p c o", p=P)
    twice = [nc.dram_tensor(f"k_twice{u}", (H * ROW, 1), F32, kind="Internal").ap() for u in range(2)]
    copies = [t.rearrange("(h w n) o -> w h (n o)", h=H, w=2) for t in twice]
    with ExitStack() as ctx:
        def sb(name, shape, dt=F32):
            return ctx.enter_context(nc.sbuf_tensor(name, shape, dt))

        def sem(name):
            return ctx.enter_context(nc.semaphore(name))

        u16 = sb("u16", [P, 2, RC, L], F16)
        kt = sb("kt", [P, 2, L])
        kb = sb("kb", [P, L])
        xn = sb("xn", [P, L])
        evn = sb("evn", [P, HALF + 1])
        odd = sb("odd", [P, HALF])
        fo = sb("fo", [P, 2, 4, Q])
        foT = sb("foT", [P, 2, 8, P], F16)
        sq = sb("sq", [P, 2, HALF])
        pw = sb("pw", [P, HALF])
        pT = sb("pT", [P, 2, 4, P], F16)
        osb = sb("osb", [P, M])
        cb = sb("cb", [P, HALF + 1])
        gb = sb("gb", [P, GATHERS, L])
        x2 = sb("x2", [P, 2, L])
        x2n = sb("x2n", [P, L])
        xT = sb("xT", [P, 2, 2, IC, P], F16)
        hs = sb("hs", [P, ER])
        hT = sb("hT", [P, 2, RC, P], F16)
        mean_of = sb("mean_of", [P, P])
        xsum = sb("xsum", [P, IC])
        xkq = sb("xkq", [P, E, IC])
        sc = sb("sc", [P, E])
        ex8 = sb("ex8", [P, E])
        soft = sb("soft", [P, 4])
        st = sb("st", [P, 12])
        mv = sb("mv", [P, 2])
        st2 = sb("st2", [P, 12])
        mv2 = sb("mv2", [P, 2])
        c1 = sb("c1", [P, 2, 2])
        n1 = sb("n1", [P, 2, 2])
        nk = sb("nk", [P, 2])
        c2 = sb("c2", [P, 2])
        n2 = sb("n2", [P, 2])
        mhalf = sb("mhalf", [P, 1])
        m8 = sb("m8", [P, 8])
        i8 = sb("i8", [P, 8], U32)
        lag = sb("lag", [P, GATHERS], U32)
        mir = sb("mir", [P, 3])
        own = sb("own", [P, 2])
        notown = sb("notown", [P, 2])
        keep = sb("keep", [P, 4])
        idx = sb("idx", [P, GATHERS], U32)
        rowbase = sb("rowbase", [P, 1], U32)
        val = sb("val", [P, 6])
        nv0 = sb("nv0", [P, 1])
        e6 = sb("e6", [P, 6])
        wsum = sb("wsum", [P, 1])
        rsum = sb("rsum", [P, 2])
        wf = sb("wfac", [P, 2, 8])

        tr = ctx.enter_context(nc.psum_tensor("tr", [P, 2, 512], F32))
        fe = ctx.enter_context(nc.psum_tensor("fe", [P, 2, 512], F32))
        acc = ctx.enter_context(nc.psum_tensor("acc", [P, 2, 512], F32))
        hps = ctx.enter_context(nc.psum_tensor("hps", [P, 512], F32))
        mean = ctx.enter_context(nc.psum_tensor("mean", [P, E], F32))

        k_loaded = [sem(f"k_loaded{u}") for u in range(2)]
        base_loaded = [sem(f"base_loaded{u}") for u in range(2)]
        doubled = [sem(f"doubled{u}") for u in range(2)]
        out_stored = [sem(f"out_stored{u}") for u in range(2)]
        down_loaded = sem("down_loaded")
        w_hi, w_lo, down_hi, down_lo, up_hi, up_lo = (
            sem(n) for n in ("w_hi", "w_lo", "down_hi", "down_lo", "up_hi", "up_lo"))
        const_ready = sem("const_ready")
        names = ("stats1 rstd1 norm1 xn_ready fold_even even_folded fold_odd1 fold_odd t1_done foT_hi "
                 "foT_lo f_done sq_done p_ready t2_done pT_hi pT_lo i_done o_copied corr_done "
                 "vals_ready wexp_done wf_ready acc0_done x2_ready stats2 rstd2 norm2 x2n_ready "
                 "t3_done xT_hi xT_lo xsum_ready down_done sc_ready mean_done smax_done sexp_done "
                 "hs_ready h_tr hT_hi hT_lo base_done acc_done out_ready").split()
        S = {n: sem(n) for n in names}
        gathered = [sem(f"gathered{s}") for s in range(GATHERS)]
        down_st = gb[:, 0:RC, :].rearrange("p a b -> p (a b)").rearrange("p (c o) -> p c o", c=IC)
        block = ctx.enter_context(nc.Block())

        FIRST, LOOP = -3, (1, 30)

        def steps(eng, step, first=FIRST):
            for i in range(first, 2 * LOOP[0]):
                step(i // 2, i % 2)
            with eng.Fori(LOOP[0], LOOP[1]) as r:
                step(r, 0)
                step(r, 1)
            for i in range(2 * LOOP[1], NT + 1):
                step(i // 2, i % 2)

        def at(r, u, i):
            return isinstance(r, int) and 2 * r + u == i

        def has(r, u, off):
            return not isinstance(r, int) or 0 <= 2 * r + u + off < NT

        def upto(eng, name, r, u, off, per=1):
            sm = S[name]
            if isinstance(r, int):
                if 2 * r + u + off >= 0:
                    eng.wait_ge(sm, per * (2 * r + u + off + 1))
            else:
                eng.wait_ge(sm, r * (2 * per) + per * (u + off + 1))

        def dma_upto(eng, sems, r, u, off, per=16):
            p, k = (u + off) % 2, (u + off) // 2
            if isinstance(r, int):
                if r + k >= 0:
                    eng.wait_ge(sems[p], per * (r + k + 1))
            else:
                eng.wait_ge(sems[p], r * per + per * (k + 1))

        @block.sync
        def _(sp):
            def number(r, mult, add):
                return mult * r + add if isinstance(r, int) else sp.snap(r * mult + add)

            def step(r, u):
                t4, t3, t2, tm = ((u + o) % 2 for o in (4, 3, 2, -1))
                row4, row2, rowm = (number(r, 2 * H, (u + o) * H) for o in (4, 2, -1))
                xn_need = number(r, 2, u + 3)
                out_need = number(r, 2, u)
                copies_need = number(r, 32, 32 * ((u + 2) // 2 + 1))
                before_need = number(r, 2, u + 2)
                if has(r, u, 4):
                    if not isinstance(r, int) or 2 * r + u + 2 >= 0:
                        sp.wait_ge(S["xn_ready"], xn_need)
                        sp.wait_ge(doubled[t4], copies_need)
                    sp.dma_start(kt[:, t4], k_rows[bass.ds(row4, H), :]).then_inc(k_loaded[t4], 16)
                if has(r, u, -1):
                    sp.wait_ge(S["out_ready"], out_need)
                    sp.dma_start(out_rows[bass.ds(rowm, H), :], x2[:, tm]).then_inc(out_stored[tm], 16)
                if has(r, u, 2):
                    if has(r, u, 1):
                        sp.wait_ge(S["acc0_done"], before_need)
                    sp.dma_start(kb[:, :], k_rows[bass.ds(row2, H), :]).then_inc(base_loaded[t2], 16)
                if has(r, u, 3):
                    for copy in range(2):
                        if has(r, u, 1):
                            sp.wait_ge(S["x2_ready"], before_need)
                        else:
                            sp.wait_ge(k_loaded[t3], 16 * ((2 * r + u + 3) // 2 + 1))
                        sp.dma_start(copies[t3][copy], kt[:, t3]).then_inc(doubled[t3], 16)

            sp.dma_start(kt[:, 0], k_rows[0:H, :]).then_inc(k_loaded[0], 16)
            sp.dma_start(down_st, down.rearrange("(c p) o -> p c o", p=P)).then_inc(down_loaded, 16)
            step(-2, 1)
            sp.dma_start(half[:, :, :], w_chunks[:, WH:IC]).then_inc(half_loaded, 16)
            step(-1, 0)
            step(-1, 1)
            sp.wait_ge(w_lo, 1)
            sp.dma_start(half[:, :, :], up.rearrange("(c p) o -> p c o", p=P)).then_inc(half_loaded, 16)
            steps(sp, step, FIRST + 3)
            for u in range(2):
                sp.wait_ge(out_stored[u], 16 * NT // 2)
                sp.wait_ge(doubled[u], 32 * NT // 2)

        @block.gpsimd
        def _(pool):
            G = nc.gpsimd
            G.memset(mean_of[:, :], 1.0 / H).then_inc(const_ready, 1)
            G.memset(mhalf[:, :], -0.5).then_inc(const_ready, 1)
            G.iota(rowbase[:, :], [[0, 1]], base=0, channel_multiplier=ROW).then_inc(const_ready, 1)
            pool.wait_ge(const_ready, 3)

            def step(r, u):
                if has(r, u, 1):
                    if at(r, u, -1):
                        pool.wait_ge(down_lo, 1)
                    dma_upto(pool, doubled, r, u, 1, 32)
                    upto(pool, "x2_ready", r, u, 0)
                    upto(pool, "vals_ready", r, u, 1)
                    G.tensor_tensor(idx[:, :], lag[:, :], rowbase[:, :].broadcast_to([P, GATHERS]), ALU.add)
                    pool.drain()
                    for s in range(GATHERS):
                        G.indirect_dma_start(gb[:, s], None, twice[(u + 1) % 2],
                                             bass.IndirectOffsetOnAxis(ap=idx[:, s:s + 1], axis=0))\
                            .then_inc(gathered[s], 16)
                if has(r, u, 3):
                    a = (u + 3) % 2
                    upto(pool, "stats1", r, u, 3)
                    G.tensor_tensor(n1[:, a, 0:1], c1[:, a, 0:1], mhalf[:, :], ALU.pow).then_inc(S["rstd1"], 1)
                    upto(pool, "rstd1", r, u, 3)
                    G.tensor_tensor(n1[:, a, 1:2], c1[:, a, 1:2], n1[:, a, 0:1], ALU.mult).then_inc(S["norm1"], 1)
                if has(r, u, 3):
                    upto(pool, "xn_ready", r, u, 3)
                    G.tensor_tensor(odd[:, 1:HALF], xn[:, 1:HALF], xn[:, L - 1:HALF:-1], ALU.subtract)\
                        .then_inc(S["fold_odd1"], 1)
                if has(r, u, 2):
                    upto(pool, "t2_done", r, u, 1)
                    upto(pool, "sq_done", r, u, 2)
                    G.tensor_tensor(pw[:, :], sq[:, 0], sq[:, 1], ALU.add).then_inc(S["p_ready"], 1)
                if has(r, u, 3):
                    upto(pool, "fold_odd1", r, u, 3)
                    upto(pool, "t1_done", r, u, 1)
                    lo, hi = odd[:, 1:Q + 1], odd[:, HALF - 1:Q - 1:-1]
                    G.tensor_tensor(fo[:, a, 2], lo, hi, ALU.subtract).then_inc(S["fold_odd"], 1)
                    G.tensor_tensor(fo[:, a, 3], lo, hi, ALU.add).then_inc(S["fold_odd"], 1)
                if has(r, u, 1):
                    upto(pool, "stats2", r, u, 1)
                    G.tensor_tensor(n2[:, 0:1], c2[:, 0:1], mhalf[:, :], ALU.pow).then_inc(S["rstd2"], 1)
                    upto(pool, "rstd2", r, u, 1)
                    G.tensor_tensor(n2[:, 1:2], c2[:, 1:2], n2[:, 0:1], ALU.mult).then_inc(S["norm2"], 1)
            steps(pool, step)

        @block.scalar
        def _(act):
            A = nc.scalar.activation
            def step(r, u):
                if has(r, u, 1):
                    upto(act, "vals_ready", r, u, 1)
                    A(e6[:, :], val[:, :], ACT.Exp, bias=nv0[:, :], accum_out=wsum[:, :]).then_inc(S["wexp_done"], 1)
                if at(r, u, 0):
                    act.wait_ge(half_loaded, 48)
                    A(u16[:, 0], half[:, :, :], ACT.Copy, scale=scale[:, 2:3]).then_inc(up_hi, 1)
                if has(r, u, 2):
                    upto(act, "f_done", r, u, 1)
                    upto(act, "t1_done", r, u, 2)
                    A(foT[:, 0].rearrange("p c h -> p (c h)"), tr[:, :, :].rearrange("p a b -> p (a b)"), ACT.Copy)\
                        .then_inc(S["foT_hi"], 1)
                if has(r, u, 0):
                    upto(act, "smax_done", r, u, 0)
                    A(ex8[:, :], mean[:, :], ACT.Exp, scale=SCORE, bias=soft[:, 1:2],
                      accum_out=soft[:, 2:3]).then_inc(S["sexp_done"], 1)
                if has(r, u, 1):
                    t = (u + 1) % 2
                    upto(act, "wf_ready", r, u, 1)
                    dma_upto(act, base_loaded, r, u, 1)
                    dma_upto(act, out_stored, r, u, -1)
                    A(x2[:, t], kb[:, :], ACT.Identity, scale=wf[:, t, 6:7], bias=wf[:, t, 7:8])\
                        .then_inc(S["acc0_done"], 1)
                if has(r, u, 3):
                    a = (u + 3) % 2
                    upto(act, "norm1", r, u, 3)
                    upto(act, "fold_even", r, u, 2)
                    upto(act, "fold_odd1", r, u, 2)
                    A(xn[:, :], kt[:, a], ACT.Identity, scale=n1[:, a, 0:1], bias=n1[:, a, 1:2])\
                        .then_inc(S["xn_ready"], 1)
                if at(r, u, -2):
                    act.wait_ge(down_loaded, 16)
                    A(d16[:, 0], down_st, ACT.Copy, scale=scale[:, 1:2]).then_inc(down_hi, 1)
                if has(r, u, 2):
                    upto(act, "p_ready", r, u, 1)
                    upto(act, "f_done", r, u, 2)
                    A(sq[:, :, :], fe[:, :, :], ACT.Square, scale=1.0 / 32).then_inc(S["sq_done"], 1)
                if has(r, u, 0):
                    upto(act, "acc_done", r, u, -1)
                    upto(act, "h_tr", r, u, 0)
                    A(hT[:, 0].rearrange("p c h -> p (c h)"), tr[:, 1], ACT.Copy).then_inc(S["hT_hi"], 1)
                if has(r, u, 2):
                    upto(act, "i_done", r, u, 1)
                    upto(act, "t2_done", r, u, 2)
                    A(pT[:, 0].rearrange("p c h -> p (c h)"), tr[:, 0], ACT.Copy).then_inc(S["pT_hi"], 1)
                if at(r, u, -2):
                    act.wait_ge(half_loaded, 32)
                    A(w16[:, 0, WH:IC], half[:, :, :], ACT.Copy, scale=scale[:, 0:1]).then_inc(w_hi, 1)
                if has(r, u, 1):
                    upto(act, "norm2", r, u, 1)
                    upto(act, "t3_done", r, u, 0)
                    t = (u + 1) % 2
                    A(x2n[:, :], x2[:, t], ACT.Identity, scale=n2[:, 0:1], bias=n2[:, 1:2]).then_inc(S["x2n_ready"], 1)
                if has(r, u, 2):
                    upto(act, "corr_done", r, u, 1)
                    upto(act, "i_done", r, u, 2)
                    A(osb[:, :], fe[:, 1, 0:M], ACT.Copy).then_inc(S["o_copied"], 1)
                if has(r, u, 1):
                    t = (u + 1) % 2
                    upto(act, "base_done", r, u, -1)
                    upto(act, "t3_done", r, u, 1)
                    A(xT[:, t, 0].rearrange("p c h -> p (c h)"), tr[:, :, :].rearrange("p a b -> p (a b)"), ACT.Copy)\
                        .then_inc(S["xT_hi"], 1)
            steps(act, step)

        @block.vector
        def _(dve):
            V = nc.vector

            def ts(out, in0, a, b=None, op0=ALU.mult, op1=ALU.bypass):
                return V.tensor_scalar(out, in0, a, b, op0, op1)

            stt = V.scalar_tensor_tensor

            LOW_PARTS_AT = 4

            dve.wait_ge(const_ready, 3)

            def stats(src, st_, mv_, c_, name):
                V.bn_stats(st_[:, 0:6], src[:, 0:512])
                V.bn_stats(st_[:, 6:12], src[:, 512:1024])
                dve.drain()
                V.bn_aggr(mv_[:, :], st_[:, :])
                dve.drain()
                ts(c_[:, 0:1], mv_[:, 1:2], LN_EPS, None, ALU.add)
                ts(c_[:, 1:2], mv_[:, 0:1], -1.0)
                dve.drain().then_inc(S[name], 1)

            def low_parts(r, u):
                if has(r, u, 0):
                    upto(dve, "hT_hi", r, u, 0)
                    V.tensor_tensor(hT[:, 1].rearrange("p c h -> p (c h)"), tr[:, 1],
                                    hT[:, 0].rearrange("p c h -> p (c h)"), ALU.subtract).then_inc(S["hT_lo"], 1)
                if has(r, u, 2):
                    upto(dve, "pT_hi", r, u, 2)
                    V.tensor_tensor(pT[:, 1].rearrange("p c h -> p (c h)"), tr[:, 0],
                                    pT[:, 0].rearrange("p c h -> p (c h)"), ALU.subtract).then_inc(S["pT_lo"], 1)

            def step(r, u):
                if has(r, u, -1):
                    upto(dve, "acc_done", r, u, -1)
                    t = (u - 1) % 2
                    stt(x2[:, t], acc[:, :, :].rearrange("p a b -> p (a b)"), scale[:, 3:4], x2[:, t],
                        ALU.mult, ALU.add).then_inc(S["out_ready"], 1)
                if has(r, u, 0):
                    V.tensor_reduce(xsum[:, :], tr[:, :, :].rearrange("p a (c h) -> p (a c) h", h=P), axis=AX,
                                    op=ALU.add)\
                        .then_inc(S["xsum_ready"], 1)
                    dve.drain()
                    V.tensor_tensor(xkq[:, :, :], kq[:, :, :].rearrange("p c e -> p e c"),
                                    xsum[:, :].unsqueeze(1).broadcast_to([P, E, IC]), ALU.mult)
                    dve.drain()
                    V.tensor_reduce(sc[:, :], xkq[:, :, :], axis=AX, op=ALU.add).then_inc(S["sc_ready"], 1)
                if has(r, u, 1):
                    V.tensor_copy(nk[:, :], n1[:, (u + 1) % 2])
                    dve.drain()
                if has(r, u, 3):
                    a = (u + 3) % 2
                    dma_upto(dve, k_loaded, r, u, 3)
                    stats(kt[:, a], st, mv, c1[:, a], "stats1")
                if has(r, u, 1):
                    t = (u + 1) % 2
                    upto(dve, "wexp_done", r, u, 1)
                    V.reciprocal(rsum[:, 0:1], wsum[:, :])
                    dve.drain()
                    V.tensor_tensor(rsum[:, 1:2], rsum[:, 0:1], nk[:, 0:1], ALU.mult)
                    dve.drain()
                    ts(wf[:, t, 0:6], e6[:, :], rsum[:, 1:2])
                    ts(wf[:, t, 6:7], e6[:, 5:6], rsum[:, 1:2], 1.0, ALU.mult, ALU.add)
                    V.tensor_copy(wf[:, t, 7:8], nk[:, 1:2])
                    dve.drain().then_inc(S["wf_ready"], 1)
                if has(r, u, 0):
                    upto(dve, "mean_done", r, u, 0)
                    V.tensor_reduce(soft[:, 0:1], mean[:, :], axis=AX, op=ALU.max)
                    dve.drain()
                    ts(soft[:, 1:2], soft[:, 0:1], -SCORE).then_inc(S["smax_done"], 1)
                if has(r, u, 2):
                    upto(dve, "foT_hi", r, u, 2)
                    V.tensor_tensor(foT[:, 1].rearrange("p c h -> p (c h)"), tr[:, :, :].rearrange("p a b -> p (a b)"),
                                    foT[:, 0].rearrange("p c h -> p (c h)"), ALU.subtract).then_inc(S["foT_lo"], 1)
                if at(r, u, -2):
                    dve.wait_ge(down_hi, 1)
                    stt(d16[:, 1], down_st, scale[:, 1:2], d16[:, 0], ALU.mult, ALU.subtract).then_inc(down_lo, 1)
                if has(r, u, 0):
                    upto(dve, "sexp_done", r, u, 0)
                    V.reciprocal(soft[:, 3:4], soft[:, 2:3])
                    dve.drain()
                    upto(dve, "h_tr", r, u, -1)
                    upto(dve, "down_done", r, u, 0)
                    stt(hs[:, :].rearrange("p (e r) -> p e r", e=E), hps[:, :].rearrange("p (e r) -> p e r", e=E),
                        soft[:, 3:4], ex8[:, :].unsqueeze(2).broadcast_to([P, E, R]), ALU.mult, ALU.mult)\
                        .then_inc(S["hs_ready"], 1)
                if has(r, u, 1):
                    t = (u + 1) % 2
                    upto(dve, "acc0_done", r, u, 1)
                    for s in range(GATHERS):
                        if s == LOW_PARTS_AT and at(r, u, -1):
                            dve.wait_ge(w_hi, 1)
                            stt(w16[:, 1, WH:IC], half[:, :, :], scale[:, 0:1], w16[:, 0, WH:IC],
                                ALU.mult, ALU.subtract).then_inc(w_lo, 1)
                        if s == LOW_PARTS_AT:
                            low_parts(r, u)
                        if isinstance(r, int):
                            dve.wait_ge(gathered[s], 16 * (2 * r + u + 2))
                        else:
                            dve.wait_ge(gathered[s], r * 32 + 16 * (u + 2))
                        last = stt(x2[:, t], gb[:, s], wf[:, t, s:s + 1], x2[:, t], ALU.mult, ALU.add)
                        if s < GATHERS - 1:
                            dve.drain()
                    last.then_inc(S["x2_ready"], 1)
                if not has(r, u, 1):
                    low_parts(r, u)
                if has(r, u, 1):
                    dve.drain()
                    stats(x2[:, (u + 1) % 2], st2, mv2, c2, "stats2")
                if at(r, u, 0):
                    dve.wait_ge(up_hi, 1)
                    for c in range(RC):
                        stt(u16[:, 1, c], half[:, c], scale[:, 2:3], u16[:, 0, c], ALU.mult, ALU.subtract)\
                            .then_inc(up_lo, 1)
                if has(r, u, 3):
                    a = (u + 3) % 2
                    upto(dve, "xn_ready", r, u, 3)
                    V.tensor_tensor(evn[:, 1:HALF], xn[:, 1:HALF], xn[:, L - 1:HALF:-1], ALU.add)
                    V.tensor_copy(evn[:, 0:HALF + 1:HALF], xn[:, 0:HALF + 1:HALF])
                    dve.drain().then_inc(S["fold_even"], 1)
                    upto(dve, "t1_done", r, u, 1)
                    lo, hi = evn[:, 0:Q], evn[:, HALF:Q:-1]
                    V.tensor_tensor(fo[:, a, 0], lo, hi, ALU.add)
                    V.tensor_tensor(fo[:, a, 1], lo, hi, ALU.subtract)
                    dve.drain().then_inc(S["even_folded"], 1)
                if has(r, u, 2):
                    upto(dve, "o_copied", r, u, 2)
                    V.tensor_tensor(cb[:, 0:M], fe[:, 0, 0:M], osb[:, :], ALU.add)
                    V.tensor_tensor(cb[:, HALF:Q:-1], fe[:, 0, 0:Q], osb[:, 0:Q], ALU.subtract)
                    dve.drain().then_inc(S["corr_done"], 1)
                    V.max(m8[:, :], cb[:, 1:HALF + 1])
                    dve.drain()
                    V.max_index(i8[:, :], m8[:, :], cb[:, 1:HALF + 1])
                if has(r, u, 1):
                    t = (u + 1) % 2
                    upto(dve, "xT_hi", r, u, 1)
                    V.tensor_tensor(xT[:, t, 1].rearrange("p c h -> p (c h)"), tr[:, :, :].rearrange("p a b -> p (a b)"),
                                    xT[:, t, 0].rearrange("p c h -> p (c h)"), ALU.subtract).then_inc(S["xT_lo"], 1)
                if has(r, u, 2):
                    dve.drain()
                    ts(lag[:, 0:3], i8[:, 0:3], 1.0, None, ALU.add)
                    ts(mir[:, :], i8[:, 0:3], -1.0, float(L - 1), ALU.mult, ALU.add)
                    ts(own[:, :], i8[:, 0:2], float(HALF - 1), None, ALU.is_equal)
                    dve.drain()
                    ts(notown[:, :], own[:, :], -1.0, 1.0, ALU.mult, ALU.add)
                    dve.drain()
                    V.tensor_tensor(keep[:, 0:2], notown[:, :], mir[:, 0:2], ALU.mult)
                    V.tensor_tensor(keep[:, 2:4], notown[:, :], m8[:, 0:2], ALU.mult)
                    V.tensor_copy(val[:, 0:3], m8[:, 0:3])
                    V.tensor_copy(val[:, 5:6], cb[:, 0:1])
                    ts(nv0[:, :], cb[:, 0:1], -1.0)
                    dve.drain()
                    stt(lag[:, 3:5], own[:, :], mir[:, 2:3], keep[:, 0:2], ALU.mult, ALU.add)
                    stt(val[:, 3:5], own[:, :], m8[:, 2:3], keep[:, 2:4], ALU.mult, ALU.add)
                    dve.drain().then_inc(S["vals_ready"], 1)
            steps(dve, step)

        @block.tensor
        def _(pe):
            mm = nc.tensor.matmul
            PASSES = ((0, 0), (0, 1), (1, 0))

            def down_product(x):
                for c in range(IC):
                    for a, b in PASSES:
                        first, last = c == 0 and (a, b) == (0, 0), c == IC - 1 and a == 1
                        m = mm(hps[:, :], x[:, a, c], d16[:, b, c], start=first, stop=last)
                return m

            def base(x, chunks):
                for c in chunks:
                    for a, b in PASSES:
                        for o in range(2):
                            m = mm(acc[:, o], x[:, a, c], w16[:, b, c, o * 512:(o + 1) * 512],
                                   start=c == 0 and (a, b) == (0, 0), stop=False, skip_group_check=True)
                return m

            def lora_up(chunks):
                for c in chunks:
                    for a, b in PASSES:
                        for o in range(2):
                            m = mm(acc[:, o], hT[:, a, c], u16[:, b, c, o * 512:(o + 1) * 512],
                                   start=False, stop=c == RC - 1 and a == 1, skip_group_check=True)
                return m

            def forward():
                for part in range(4):
                    for c in range(2):
                        for a, b in PASSES:
                            m = mm(fe[:, part // 2, (part % 2) * Q:(part % 2 + 1) * Q], foT[:, a, 2 * part + c],
                                   fwd[:, b, 2 * part + c], start=c == 0 and (a, b) == (0, 0), stop=c == 1 and a == 1)
                return m

            def backward():
                for part in range(2):
                    for c in range(2):
                        for a, b in PASSES:
                            m = mm(fe[:, part, 0:MS], pT[:, a, 2 * part + c], inv[:, b, 2 * part + c],
                                   start=c == 0 and (a, b) == (0, 0), stop=c == 1 and a == 1)
                return m

            def transposes(dst, src, count):
                for c in range(count):
                    m = nc.tensor.transpose(dst[:, c * P:(c + 1) * P], src[:, c * P:(c + 1) * P], ident[:, :])
                return m

            tr_flat = tr[:, :, :].rearrange("p a b -> p (a b)")
            pe.wait_ge(const_ready, 3)

            def step(r, u):
                x = xT[:, u]
                if at(r, u, 0):
                    pe.wait_ge(down_lo, 1)
                if has(r, u, 0):
                    upto(pe, "xT_lo", r, u, 0)
                    upto(pe, "hs_ready", r, u, -1)
                    down_product(x).then_inc(S["down_done"], 1)
                if has(r, u, 2):
                    a = (u + 2) % 2
                    upto(pe, "fold_odd", r, u, 2, 2)
                    upto(pe, "even_folded", r, u, 2)
                    upto(pe, "xsum_ready", r, u, 0)
                    transposes(tr_flat, fo[:, a].rearrange("p a b -> p (a b)"), 8).then_inc(S["t1_done"], 1)
                if has(r, u, 0):
                    upto(pe, "sc_ready", r, u, 0)
                    mm(mean[:, :], mean_of[:, :], sc[:, :], start=True, stop=True).then_inc(S["mean_done"], 1)
                    upto(pe, "out_ready", r, u, -1)
                    base(x, range(0, 3))
                if has(r, u, 2):
                    upto(pe, "foT_lo", r, u, 2)
                    upto(pe, "corr_done", r, u, 1)
                    forward().then_inc(S["f_done"], 1)
                if at(r, u, 0):
                    pe.wait_ge(w_lo, 1)
                if has(r, u, 0):
                    base(x, range(3, 5))
                    upto(pe, "hs_ready", r, u, 0)
                    if has(r, u, 2):
                        upto(pe, "foT_lo", r, u, 2)
                    transposes(tr[:, 1], hs[:, :], RC).then_inc(S["h_tr"], 1)
                if has(r, u, 2):
                    upto(pe, "p_ready", r, u, 2)
                    transposes(tr[:, 0], pw[:, :], 4).then_inc(S["t2_done"], 1)
                if has(r, u, 0):
                    base(x, range(5, IC)).then_inc(S["base_done"], 1)
                if has(r, u, 2):
                    upto(pe, "pT_lo", r, u, 2)
                    upto(pe, "sq_done", r, u, 2)
                    backward().then_inc(S["i_done"], 1)
                if has(r, u, 0):
                    upto(pe, "hT_lo", r, u, 0)
                    for c in range(0, RC // 2):
                        if at(r, u, 0):
                            pe.wait_ge(up_lo, c + 1)
                        lora_up([c])
                if has(r, u, 1):
                    upto(pe, "x2n_ready", r, u, 1)
                    if has(r, u, 2):
                        upto(pe, "pT_lo", r, u, 2)
                    if has(r, u, 0):
                        upto(pe, "hT_lo", r, u, 0)
                    transposes(tr_flat, x2n[:, :], 8).then_inc(S["t3_done"], 1)
                if at(r, u, 0):
                    pe.wait_ge(up_lo, RC)
                if has(r, u, 0):
                    lora_up(range(RC // 2, RC)).then_inc(S["acc_done"], 1)
            steps(pe, step)


def kernel(**inputs):
    import concourse.bacc as bacc
    from concourse.bass_utils import run_bass_kernel_spmd

    x = inputs["x"]
    part = np.transpose(x, (3, 2, 1, 0))
    fwd_c, inv_c = dft_constants()
    down = np.transpose(inputs["L0_ffn_lora_down"], (1, 0, 2)).reshape(L, ER)
    arrays = {
        "w_re": np.concatenate([part[0], part[0]]), "w_im": np.concatenate([part[1], part[1]]),
        "log_dt": inputs["L0_tok_log_dt"].T,
        "lam": np.concatenate([inputs["L0_tok_Lambda"]] * 2),
        "w_org": inputs["L0_ffn_W_org"].T, "down": down,
        "up": inputs["L0_ffn_lora_up"].reshape(ER, L), "keys": inputs["L0_ffn_lora_keys"].T,
        "wq": inputs["L0_ffn_Wq"],
        "fwd": fwd_c, "inv": inv_c, "eye": np.eye(P, dtype=np.float32),
    }
    arrays = {k: np.ascontiguousarray(a) for k, a in arrays.items()}
    nc = bacc.Bacc("TRN2", target_bir_lowering=False, num_devices=1)
    args = [nc.dram_tensor(f"in_{k}", a.shape, mybir.dt.from_np(a.dtype), kind="ExternalInput").ap()
            for k, a in arrays.items()]
    out = nc.dram_tensor("out", (NT, H, L), F32, kind="ExternalOutput").ap()
    vit_tower(nc, *args, out)
    r = run_bass_kernel_spmd(nc, [{f"in_{k}": a for k, a in arrays.items()}], core_ids=[0])
    return r.results[0]["out"]
```
